# Optimizing a Trainium2 kernel written in Bass

```python
import numpy as np
import jax
import jax.numpy as jnp

def _softmax(x, axis=-1):
    return jax.nn.softmax(x, axis=axis)

def _gelu(x):
    return jax.nn.gelu(x, approximate=True)

def _silu(x):
    return jax.nn.silu(x)

def _sigmoid(x):
    return jax.nn.sigmoid(x)

def _layernorm(x, axis=-1, eps=1e-05):
    m = jnp.mean(x, axis=axis, keepdims=True)
    v = jnp.var(x, axis=axis, keepdims=True)
    return (x - m) / jnp.sqrt(v + eps)

def _scatter_add(tgt, idx, src, axis=0):
    return tgt.at[idx].add(src)

def _segment_sum(src, seg, n):
    return jax.ops.segment_sum(src, seg, n)
kernel_name = 'mk_cond_resid_d4_seqx_r8_9d1346'

def setup_inputs(seed: int=0):
    np.random.seed(seed)
    _w = jnp.asarray

    def _rec_inputs():
        import jax
        import jax.numpy as jnp
        _rk = jax.random.key(seed)
        x = -0.0003929 + 0.9999 * jax.random.normal(jax.random.fold_in(_rk, 1), (16, 128, 256), jnp.float32)
        _lenS = 128 - jax.random.randint(jax.random.fold_in(_rk, 7), (16,), 0, max(1, 128 // 4) + 1, jnp.int32)
        _lenS2 = 128 - jax.random.randint(jax.random.fold_in(_rk, 8), (16,), 0, max(1, 128 // 4) + 1, jnp.int32)
        cond_2048 = 0.00782532 + 1.00527 * jax.random.normal(jax.random.fold_in(_rk, 11), (16, 256), jnp.float32)
        return (x, cond_2048)
    x, cond_2048 = _rec_inputs()

    def _L0_cond_setup():
        import jax, jax.numpy as jnp
        import numpy as np
        HEADS = 16
        EPS = 1e-06

        def _rms_norm(x, g):
            xf = x.astype(jnp.float32)
            y = xf * jax.lax.rsqrt(jnp.mean(xf * xf, axis=-1, keepdims=True) + EPS)
            return y.astype(x.dtype) * g
        key = jax.random.key(seed)
        ks = jax.random.split(key, 6)
        b, n, dim, emb_dim = (4, 256, 256, 256)
        d_head = dim // HEADS
        return {'x': jax.random.normal(ks[0], (b, n, dim), jnp.float32), 'emb': jax.random.normal(ks[1], (b, 1, emb_dim), jnp.float32), 'W_emb': jax.random.normal(ks[2], (emb_dim, 2 * dim), jnp.float32) * emb_dim ** (-0.5), 'b_emb': jnp.zeros((2 * dim,), jnp.float32), 'g_norm': jnp.ones((dim,), jnp.float32), 'W_qkv': jax.random.normal(ks[3], (dim, 3 * dim), jnp.float32) * dim ** (-0.5), 'g_q': jnp.ones((d_head,), jnp.float32), 'g_k': jnp.ones((d_head,), jnp.float32), 'W_out': jax.random.normal(ks[4], (dim, dim), jnp.float32) * dim ** (-0.5)}
    _L0_cond_all = _L0_cond_setup()
    _L0_cond_in = {k: v for k, v in _L0_cond_all.items() if k in ('W_emb', 'b_emb', 'g_norm', 'W_qkv', 'g_q', 'g_k', 'W_out')}
    del _L0_cond_all

    def _L1_cond_setup():
        import jax, jax.numpy as jnp
        import numpy as np
        DT = 0.01
        EPSILON = 0.08
        ALPHA = 0.7
        BETA = 0.8
        CLAMP = 20.0
        B, T, N = (32, 128, 256)

        def _derivative(q, p, drive, coupling, bias):
            i_couple = jnp.tanh(q) @ coupling.T
            dq = q - q ** 3 / 3.0 - p + drive + i_couple + bias
            dp = EPSILON * (q + ALPHA - BETA * p)
            return (dq, dp)

        def _rk4_step(q, p, drive, coupling, bias):
            dq1, dp1 = _derivative(q, p, drive, coupling, bias)
            dq2, dp2 = _derivative(q + 0.5 * DT * dq1, p + 0.5 * DT * dp1, drive, coupling, bias)
            dq3, dp3 = _derivative(q + 0.5 * DT * dq2, p + 0.5 * DT * dp2, drive, coupling, bias)
            dq4, dp4 = _derivative(q + DT * dq3, p + DT * dp3, drive, coupling, bias)
            q_next = q + DT / 6.0 * (dq1 + 2 * dq2 + 2 * dq3 + dq4)
            p_next = p + DT / 6.0 * (dp1 + 2 * dp2 + 2 * dp3 + dp4)
            q_next = jnp.clip(q_next, -CLAMP, CLAMP)
            p_next = jnp.clip(p_next, -CLAMP, CLAMP)
            return (q_next, p_next)
        key = jax.random.key(seed)
        k1, k2, k3, k4 = jax.random.split(key, 4)
        return {'q0': jax.random.normal(k1, (B, N), dtype=jnp.float32), 'p0': jax.random.normal(k2, (B, N), dtype=jnp.float32), 'input_drive_seq': jax.random.normal(k3, (B, T, N), dtype=jnp.float32), 'coupling': jax.random.normal(k4, (N, N), dtype=jnp.float32) * 0.01, 'bias': jnp.zeros((N,), dtype=jnp.float32)}
    _L1_cond_all = _L1_cond_setup()
    _L1_cond_in = {k: v for k, v in _L1_cond_all.items() if k in ('coupling', 'bias')}
    del _L1_cond_all

    def _L2_cond_setup():
        import jax, jax.numpy as jnp
        import numpy as np
        DIM = 256
        H = 16
        DH = 128
        INNER = H * DH
        MLP = 4 * DIM
        B, T = (2, 256)
        EPS = 1e-06

        def _ln(x):
            mu = jnp.mean(x, axis=-1, keepdims=True)
            var = jnp.var(x, axis=-1, keepdims=True)
            return (x - mu) * jax.lax.rsqrt(var + EPS)
        key = jax.random.key(seed)
        ks = jax.random.split(key, 12)
        s = 0.02
        return {'x': jax.random.normal(ks[0], (B, T, DIM), jnp.float32), 'timestep_embed': jax.random.normal(ks[1], (B, DIM), jnp.float32), 'ada_w': jax.random.normal(ks[2], (DIM, 6 * DIM), jnp.float32) * s, 'ada_b': jnp.zeros((6 * DIM,), jnp.float32), 'qkv_w': jax.random.normal(ks[3], (DIM, 3 * INNER), jnp.float32) * s, 'qkv_b': jnp.zeros((3 * INNER,), jnp.float32), 'out_w': jax.random.normal(ks[4], (INNER, DIM), jnp.float32) * s, 'out_b': jnp.zeros((DIM,), jnp.float32), 'ffn_w1': jax.random.normal(ks[5], (DIM, MLP), jnp.float32) * s, 'ffn_b1': jnp.zeros((MLP,), jnp.float32), 'ffn_w2': jax.random.normal(ks[6], (MLP, DIM), jnp.float32) * s, 'ffn_b2': jnp.zeros((DIM,), jnp.float32)}
    _L2_cond_all = _L2_cond_setup()
    _L2_cond_in = {k: v for k, v in _L2_cond_all.items() if k in ('ada_w', 'ada_b', 'qkv_w', 'qkv_b', 'out_w', 'out_b', 'ffn_w1', 'ffn_b1', 'ffn_w2', 'ffn_b2')}
    del _L2_cond_all

    def _L3_cond_setup():
        import jax, jax.numpy as jnp
        import numpy as np
        B, T, D = (16, 128, 256)
        key = jax.random.key(seed)
        k0, k1, k2, k3 = jax.random.split(key, 4)
        scale = 1.0 / np.sqrt(D)
        return {'initial_state': jax.random.normal(k0, (B, D), jnp.float32), 'inputs': jax.random.normal(k1, (B, T, D), jnp.float32), 'W_ih': jax.random.normal(k2, (D, 3 * D), jnp.float32) * scale, 'W_hh': jax.random.normal(k3, (D, 3 * D), jnp.float32) * scale, 'b_ih': jnp.zeros((3 * D,), jnp.float32), 'b_hh': jnp.zeros((3 * D,), jnp.float32)}
    _L3_cond_all = _L3_cond_setup()
    _L3_cond_in = {k: v for k, v in _L3_cond_all.items() if k in ('W_ih', 'W_hh', 'b_ih', 'b_hh')}
    del _L3_cond_all
    return {'x': x, 'cond_2048': cond_2048, 'L0_cond_W_emb': _L0_cond_in['W_emb'], 'L0_cond_b_emb': _L0_cond_in['b_emb'], 'L0_cond_g_norm': _L0_cond_in['g_norm'], 'L0_cond_W_qkv': _L0_cond_in['W_qkv'], 'L0_cond_g_q': _L0_cond_in['g_q'], 'L0_cond_g_k': _L0_cond_in['g_k'], 'L0_cond_W_out': _L0_cond_in['W_out'], 'L1_cond_coupling': _L1_cond_in['coupling'], 'L1_cond_bias': _L1_cond_in['bias'], 'L2_cond_ada_w': _L2_cond_in['ada_w'], 'L2_cond_ada_b': _L2_cond_in['ada_b'], 'L2_cond_qkv_w': _L2_cond_in['qkv_w'], 'L2_cond_qkv_b': _L2_cond_in['qkv_b'], 'L2_cond_out_w': _L2_cond_in['out_w'], 'L2_cond_out_b': _L2_cond_in['out_b'], 'L2_cond_ffn_w1': _L2_cond_in['ffn_w1'], 'L2_cond_ffn_b1': _L2_cond_in['ffn_b1'], 'L2_cond_ffn_w2': _L2_cond_in['ffn_w2'], 'L2_cond_ffn_b2': _L2_cond_in['ffn_b2'], 'L3_cond_W_ih': _L3_cond_in['W_ih'], 'L3_cond_W_hh': _L3_cond_in['W_hh'], 'L3_cond_b_ih': _L3_cond_in['b_ih'], 'L3_cond_b_hh': _L3_cond_in['b_hh']}

def reference(x, cond_2048, L0_cond_W_emb, L0_cond_b_emb, L0_cond_g_norm, L0_cond_W_qkv, L0_cond_g_q, L0_cond_g_k, L0_cond_W_out, L1_cond_coupling, L1_cond_bias, L2_cond_ada_w, L2_cond_ada_b, L2_cond_qkv_w, L2_cond_qkv_b, L2_cond_out_w, L2_cond_out_b, L2_cond_ffn_w1, L2_cond_ffn_b1, L2_cond_ffn_w2, L2_cond_ffn_b2, L3_cond_W_ih, L3_cond_W_hh, L3_cond_b_ih, L3_cond_b_hh):
    import jax
    import jax.numpy as jnp

    def _L0_cond_ref(x, emb, W_emb, b_emb, g_norm, W_qkv, g_q, g_k, W_out):
        import jax, jax.numpy as jnp
        import numpy as np
        HEADS = 16
        EPS = 1e-06

        def _rms_norm(x, g):
            xf = x.astype(jnp.float32)
            y = xf * jax.lax.rsqrt(jnp.mean(xf * xf, axis=-1, keepdims=True) + EPS)
            return y.astype(x.dtype) * g
        b, n, dim = x.shape
        h = HEADS
        d = dim // h
        scale_shift = emb @ W_emb + b_emb
        scale, shift = jnp.split(scale_shift, 2, axis=-1)
        xn = _rms_norm(x, g_norm) * (1.0 + scale) + shift
        qkv = xn @ W_qkv
        qkv = qkv.reshape(b, n, 3, h, d)
        q, k, v = jnp.moveaxis(qkv, 2, 0)
        q = jnp.swapaxes(q, 1, 2)
        k = jnp.swapaxes(k, 1, 2)
        v = jnp.swapaxes(v, 1, 2)
        q = _rms_norm(q, g_q)
        k = _rms_norm(k, g_k)
        logits = jnp.einsum('bhqd,bhkd->bhqk', q, k) * d ** (-0.5)
        attn = jax.nn.softmax(logits, axis=-1)
        o = jnp.einsum('bhqk,bhkd->bhqd', attn, v)
        o = jnp.swapaxes(o, 1, 2).reshape(b, n, dim)
        return o + o @ W_out

    def _L1_cond_ref(q0, p0, input_drive_seq, coupling, bias):
        import jax, jax.numpy as jnp
        import numpy as np
        DT = 0.01
        EPSILON = 0.08
        ALPHA = 0.7
        BETA = 0.8
        CLAMP = 20.0
        B, T, N = (32, 128, 256)

        def _derivative(q, p, drive, coupling, bias):
            i_couple = jnp.tanh(q) @ coupling.T
            dq = q - q ** 3 / 3.0 - p + drive + i_couple + bias
            dp = EPSILON * (q + ALPHA - BETA * p)
            return (dq, dp)

        def _rk4_step(q, p, drive, coupling, bias):
            dq1, dp1 = _derivative(q, p, drive, coupling, bias)
            dq2, dp2 = _derivative(q + 0.5 * DT * dq1, p + 0.5 * DT * dp1, drive, coupling, bias)
            dq3, dp3 = _derivative(q + 0.5 * DT * dq2, p + 0.5 * DT * dp2, drive, coupling, bias)
            dq4, dp4 = _derivative(q + DT * dq3, p + DT * dp3, drive, coupling, bias)
            q_next = q + DT / 6.0 * (dq1 + 2 * dq2 + 2 * dq3 + dq4)
            p_next = p + DT / 6.0 * (dp1 + 2 * dp2 + 2 * dp3 + dp4)
            q_next = jnp.clip(q_next, -CLAMP, CLAMP)
            p_next = jnp.clip(p_next, -CLAMP, CLAMP)
            return (q_next, p_next)
        drive_tbn = jnp.swapaxes(input_drive_seq, 0, 1)

        def scan_fn(carry, drive):
            q, p = carry
            q, p = _rk4_step(q, p, drive, coupling, bias)
            return ((q, p), q)
        (_, _), q_trace_tbn = jax.lax.scan(scan_fn, (q0, p0), drive_tbn)
        return jnp.swapaxes(q_trace_tbn, 0, 1)

    def _L2_cond_ref(x, timestep_embed, ada_w, ada_b, qkv_w, qkv_b, out_w, out_b, ffn_w1, ffn_b1, ffn_w2, ffn_b2):
        import jax, jax.numpy as jnp
        import numpy as np
        DIM = 256
        H = 16
        DH = 128
        INNER = H * DH
        MLP = 4 * DIM
        B, T = (2, 256)
        EPS = 1e-06

        def _ln(x):
            mu = jnp.mean(x, axis=-1, keepdims=True)
            var = jnp.var(x, axis=-1, keepdims=True)
            return (x - mu) * jax.lax.rsqrt(var + EPS)
        Bc, Tc, D = x.shape
        ada = (timestep_embed @ ada_w + ada_b)[:, None, :]
        shift1, scale1, gate1, shift2, scale2, gate2 = jnp.split(ada, 6, axis=-1)
        x1 = _ln(x) * (1.0 + scale1) + shift1
        qkv = (x1 @ qkv_w + qkv_b).reshape(Bc, Tc, 3, H, DH)
        q, k, v = (qkv[:, :, 0], qkv[:, :, 1], qkv[:, :, 2])
        scale = DH ** (-0.5)
        attn = jnp.einsum('bthd,bshd->bhts', q, k) * scale
        attn = jax.nn.softmax(attn, axis=-1)
        attn_out = jnp.einsum('bhts,bshd->bthd', attn, v).reshape(Bc, Tc, INNER)
        attn_out = attn_out @ out_w + out_b
        x = x + gate1 * attn_out
        x2 = _ln(x) * (1.0 + scale2) + shift2
        h = jax.nn.gelu(x2 @ ffn_w1 + ffn_b1, approximate=False)
        x = x + gate2 * (h @ ffn_w2 + ffn_b2)
        return x

    def _L3_cond_ref(initial_state, inputs, W_ih, W_hh, b_ih, b_hh):
        import jax, jax.numpy as jnp
        import numpy as np
        B, T, D = (16, 128, 256)
        "ScanOverTime(GRU cell): sequential per-timestep module call with\n            dict-state passing; merge_dict_trees stacks the per-step\n            'state_predicted' tensors along axis=1 -> [B, T, D]."

        def cell(h, x):
            gi = x @ W_ih + b_ih
            gh = h @ W_hh + b_hh
            i_r, i_z, i_n = jnp.split(gi, 3, axis=-1)
            h_r, h_z, h_n = jnp.split(gh, 3, axis=-1)
            r = jax.nn.sigmoid(i_r + h_r)
            z = jax.nn.sigmoid(i_z + h_z)
            n = jnp.tanh(i_n + r * h_n)
            h_new = (1.0 - z) * n + z * h
            return (h_new, h_new)
        xs = jnp.swapaxes(inputs, 0, 1)
        _, hs = jax.lax.scan(cell, initial_state, xs)
        return jnp.swapaxes(hs, 0, 1)
    x = x + _L0_cond_ref(x, cond_2048[:, None, :], L0_cond_W_emb, L0_cond_b_emb, L0_cond_g_norm, L0_cond_W_qkv, L0_cond_g_q, L0_cond_g_k, L0_cond_W_out)
    x = x + _L1_cond_ref(cond_2048, cond_2048, x, L1_cond_coupling, L1_cond_bias)
    x = x + _L2_cond_ref(x, cond_2048, L2_cond_ada_w, L2_cond_ada_b, L2_cond_qkv_w, L2_cond_qkv_b, L2_cond_out_w, L2_cond_out_b, L2_cond_ffn_w1, L2_cond_ffn_b1, L2_cond_ffn_w2, L2_cond_ffn_b2)
    x = x + _L3_cond_ref(cond_2048, x, L3_cond_W_ih, L3_cond_W_hh, L3_cond_b_ih, L3_cond_b_hh)
    return x

_drawn_inputs = setup_inputs


def setup_inputs(seed=0):
    import zlib

    import numpy as np

    out = dict(_drawn_inputs(seed))
    spreads = {'L0_cond_b_emb': (0.0, 0.1),
     'L0_cond_g_norm': (1.0, 0.2),
     'L0_cond_g_q': (1.0, 0.6),
     'L0_cond_g_k': (1.0, 0.547),
     'L1_cond_bias': (0.0, 0.343),
     'L2_cond_ada_b': (0.0, 0.8),
     'L2_cond_qkv_b': (0.0, 0.8),
     'L2_cond_out_b': (0.0, 0.8),
     'L2_cond_ffn_b1': (0.0, 0.8),
     'L2_cond_ffn_b2': (0.0, 0.8),
     'L3_cond_b_ih': (0.0, 2.0),
     'L3_cond_b_hh': (0.0, 2.0)}
    factors = {'L2_cond_qkv_w': 3.069,
     'L2_cond_out_w': 2.83,
     'L2_cond_ffn_w1': 7.203,
     'L2_cond_ffn_w2': 6.615,
     'L1_cond_coupling': 2.732,
     'L3_cond_W_hh': 4.871}
    for name, (base, spread) in spreads.items():
        noise = np.random.default_rng([zlib.crc32(name.encode()), seed]).standard_normal(out[name].shape)
        drawn = base * np.exp(spread * noise) if base else spread * noise
        out[name] = jnp.asarray(drawn.astype(out[name].dtype))
    for name, factor in factors.items():
        out[name] = (out[name] * factor).astype(out[name].dtype)
    return out
```

```python
from contextlib import ExitStack

import concourse.bass as bass
from concourse import mybir

F32 = mybir.dt.float32
F32R = mybir.dt.float32r
F16 = mybir.dt.float16
ACT = mybir.ActivationFunctionType
ALU = mybir.AluOpType
AX_X = mybir.AxisListType.X
MUL, ADD, SUB = ALU.mult, ALU.add, ALU.subtract

P = 128
B, T, D = 16, 128, 256
C = D // P
TOK = B * T
NB = TOK // 512
BB = B // NB
H0, D0 = 16, 16
H2, D2 = 16, 128
FF = 4 * D
DT, EPSILON, ALPHA, BETA, CLAMP = 0.01, 0.08, 0.7, 0.8, 20.0
EPS = 1e-6
W1 = C * B
LAP = 16
LAP3 = 16

V_GNORM, V_BEMB, V_BIAS1, V_ADAB, V_QKB, V_OUTB, V_B1, V_B2, V_GQ, V_GK, V_ROWS = (
    0, 2, 6, 8, 20, 52, 54, 62, 64, 65, 66)


class Count:

    def __init__(self, eng, sem):
        self.eng, self.sem, self.n = eng, sem, 0

    def __call__(self, ins):
        ins.then_inc(self.sem, 1)
        self.n += 1
        return self.n

    def wait(self, n):
        self.eng.wait_ge(self.sem, n)


def prepare(nc, ctx, a, g):
    sb = lambda name, shape, dt=F32: ctx.enter_context(nc.sbuf_tensor(name, shape, dt))
    sem = lambda name: ctx.enter_context(nc.semaphore(name))
    cond = sb("cond", [B, D])
    rows = sb("rows", [V_ROWS, P])
    x_tok = sb("x_tok", [P, B, D])
    xn_tok = sb("xn_tok", [P, B, D])
    square = sb("square", [P, 2, D])
    sum_sq = sb("sum_sq", [P, B])
    log_ms = sb("log_ms", [P, B])
    rstd = sb("rstd", [P, B])
    w_emb = sb("w_emb", [P, C, 2 * D])
    coup = sb("coup", [P, C, D])
    coup_abs = sb("coup_abs", [P, 1])
    coup_row = sb("coup_row", [1, P])
    coup_top = sb("coup_top", [1, 1])
    ones_row = sb("ones_row", [1, P])
    coup_inv = sb("coup_inv", [P, 1])
    coup_n = sb("coup_n", [P, C * D])
    gain = sb("gain", [P, C, B])
    d_x = [sem(f"d_x{n}") for n in range(NB)]
    d_cond, d_rows, d_emb, d_coup = sem("d_cond"), sem("d_rows"), sem("d_emb"), sem("d_coup")
    consts_made = sem("consts_made")
    pool_made = sem("pool_made")
    sq_done = sem("sq_done")
    act_chain = sem("act_chain")
    dve_chain = sem("dve_chain")
    rstd_ready = sem("rstd_ready")
    xn_ready = sem("xn_ready")
    small_full = sem("small_full")
    small_out = sem("small_out")
    xn_full, xn_out = sem("xn_full"), sem("xn_out")
    x_full, x_out = sem("x_full"), sem("x_out")
    x_in = a["x"].rearrange("b t f -> t b f")
    bank = g.bank

    with nc.Block() as block:
        @block.sync
        def _(sp):
            sp.dma_start(cond[:, :], a["cond_2048"]).then_inc(d_cond, 16)
            for n in range(NB):
                bs = slice(BB * n, BB * n + BB)
                sp.dma_start(x_tok[:, bs, :], x_in[:, bs, :]).then_inc(d_x[n], 16)
            by_chunk = lambda w: w.rearrange("(c p) n -> p c n", p=P)
            sp.dma_start(w_emb[:, :, :], by_chunk(a["L0_cond_W_emb"])).then_inc(d_emb, 16)
            sp.dma_start(coup[:, :, :], by_chunk(a["L1_cond_coupling"])).then_inc(d_coup, 16)
            sp.dma_start(g.w_qkv0[:, :, :], by_chunk(a["L0_cond_W_qkv"])).then_inc(g.d_w0, 16)
            sp.dma_start(g.w_out0[:, :, :], by_chunk(a["L0_cond_W_out"])).then_inc(g.d_w0, 16)
            sp.dma_start(g.ada_w[:, :, :], by_chunk(a["L2_cond_ada_w"])).then_inc(g.d_ada, 16)

        @block.gpsimd
        def _(pool):
            made = Count(pool, pool_made)
            G = nc.gpsimd
            made(G.memset(g.ident[:, :], 0.0))
            made(G.memset(g.mean_w[:, :], 1.0 / D))
            n = made(G.memset(g.block_w[:, :], 1.0 / D0))
            made.wait(n)
            made(G.affine_select(out=g.ident[:, :], in_=g.ident[:, :], compare_op=ALU.not_equal,
                                 fill=1.0, base=0, pattern=[[-1, P]], channel_multiplier=1))
            blocks = g.block_w[:, :].rearrange("p (h e) -> p h e", e=D0)
            n = made(G.affine_select(out=blocks, in_=blocks, compare_op=ALU.is_ge, fill=0.0, base=0,
                                     pattern=[[-D0, P // D0], [0, D0]], channel_multiplier=1))
            made.wait(n)
            n = made(G.affine_select(out=blocks, in_=blocks, compare_op=ALU.is_ge, fill=0.0,
                                     base=D0 - 1, pattern=[[D0, P // D0], [0, D0]],
                                     channel_multiplier=-1))
            made.wait(n)
            G.memset(ones_row[:, :], 1.0).then_inc(consts_made, 1)

        @block.scalar
        def _(act):
            A = nc.scalar
            row = lambda v, n: rows[v:v + n, :]
            stack = lambda w: w.rearrange("(r p) -> r p", p=P)
            for v, w in ((V_GNORM, "L0_cond_g_norm"), (V_BEMB, "L0_cond_b_emb"),
                         (V_BIAS1, "L1_cond_bias"), (V_ADAB, "L2_cond_ada_b"),
                         (V_OUTB, "L2_cond_out_b"), (V_B1, "L2_cond_ffn_b1"),
                         (V_B2, "L2_cond_ffn_b2")):
                act.dma_start(row(v, a[w].shape[0] // P), stack(a[w])).then_inc(d_rows, 16)
            act.dma_start(row(V_QKB, 2 * H2), stack(a["L2_cond_qkv_b"][0:2 * H2 * D2])).then_inc(d_rows, 16)
            for v, w in ((V_GQ, "L0_cond_g_q"), (V_GK, "L0_cond_g_k")):
                tiled = a[w].rearrange("(o e) -> o e", o=1).unsqueeze(1).broadcast_to([1, P // D0, D0])
                act.dma_start(row(v, 1).rearrange("o (h e) -> o h e", e=D0), tiled).then_inc(d_rows, 16)
            chain = Count(act, act_chain)
            for b in range(B):
                act.wait_ge(d_x[b // BB], 16)
                if b >= 2:
                    chain.wait(b - 1)
                n = chain(A.activation(square[:, b % 2, :], x_tok[:, b, :], ACT.Square,
                                       accum_out=sum_sq[:, b:b + 1]))
            chain.wait(n)
            act.wait_ge(dve_chain, 1)
            n = chain(A.activation(log_ms[:, :], sum_sq[:, :], ACT.Ln, bias=g.eps6[:, :], scale=1.0 / D))
            chain.wait(n)
            A.activation(rstd[:, :], log_ms[:, :], ACT.Exp, scale=-0.5).then_inc(rstd_ready, 1)
            for n in range(2 * NB):
                act.wait_ge(x_full, n + 1)
                A.activation(g.xT[:, n // NB, BB * (n % NB):BB * (n % NB) + BB, :],
                             bank[4 + n % 2][:, :], ACT.Copy).then_inc(x_out, 1)

        @block.vector
        def _(dve):
            V = nc.vector
            chain = Count(dve, dve_chain)
            chain(V.memset(g.eps6[:, :], EPS))
            dve.wait_ge(small_full, 1)
            V.tensor_copy(g.condT[:, :, :], bank[0][:, 0:W1]).then_inc(small_out, 1)
            dve.wait_ge(small_full, 2)
            V.tensor_copy(g.vec[:, :], bank[1][:, 0:V_ROWS]).then_inc(small_out, 1)
            dve.wait_ge(d_coup, 16)
            V.tensor_reduce(coup_abs[:, :], coup[:, :, :].rearrange("p c n -> p (c n)"), op=ALU.max,
                            axis=AX_X, apply_absolute_value=True).then_inc(small_out, 1)
            dve.wait_ge(small_full, 4)
            V.tensor_reduce(coup_top[:, :], bank[3][0:1, 0:P], op=ALU.max, axis=AX_X).then_inc(small_out, 1)
            dve.wait_ge(small_full, 5)
            n = chain(V.tensor_scalar(g.coup_scale[:, 3:4], bank[0][:, 0:1], 1e-30, None, ALU.max))
            chain.wait(n)
            for i, step in enumerate((DT / 2, DT, DT / 6)):
                chain(V.tensor_scalar(g.coup_scale[:, i:i + 1], g.coup_scale[:, 3:4], step, None, MUL))
            n = chain(V.reciprocal(coup_inv[:, :], g.coup_scale[:, 3:4]))
            chain.wait(n)
            n = chain(V.tensor_scalar(coup_n[:, :], bank[2][:, :], coup_inv[:, 0:1], None, MUL))
            chain.wait(n)
            n = chain(V.tensor_copy(g.coup_hi[:, :], coup_n[:, :]))
            chain.wait(n)
            chain(V.tensor_tensor(g.coup_lo[:, :], coup_n[:, :], g.coup_hi[:, :], SUB))
            dve.wait_ge(small_full, 6)
            for m in range(2 * C):
                src = bank[1][:, B * m:B * m + B]
                bias = g.vec[:, V_BEMB + m:V_BEMB + m + 1]
                if m < C:
                    n = chain(V.tensor_scalar(gain[:, m, :], src, bias, 1.0, ADD, ADD))
                else:
                    chain(V.tensor_scalar(g.shift0[:, m - C, :], src, bias, None, ADD))
            chain.wait(n)
            for c in range(C):
                n = chain(V.tensor_scalar(g.gain0[:, c, :], gain[:, c, :],
                                          g.vec[:, V_GNORM + c:V_GNORM + c + 1], None, MUL))
            dve.wait_ge(rstd_ready, 1)
            for b in range(B):
                V.tensor_scalar(xn_tok[:, b, :], x_tok[:, b, :], rstd[:, b:b + 1], None,
                                MUL).then_inc(xn_ready, 1)
            chain.wait(n)
            for n in range(2 * NB):
                dve.wait_ge(xn_full, n + 1)
                c = n // NB
                for i in range(BB):
                    b = BB * (n % NB) + i
                    last = V.tensor_scalar(g.xm[:, c, b, :], bank[6 + n % 2][:, P * i:P * i + P],
                                           g.gain0[:, c, b:b + 1], g.shift0[:, c, b:b + 1], MUL, ADD)
                last.then_inc(xn_out, 1)

        @block.tensor
        def _(pe):
            M = nc.tensor
            pe.wait_ge(pool_made, 4)
            pe.wait_ge(d_cond, 16)
            for c in range(C):
                last = M.transpose(bank[0][:, B * c:B * c + B], cond[:, P * c:P * c + P], g.ident[0:B, 0:B])
            last.then_inc(small_full, 1)
            pe.wait_ge(d_rows, 16 * 10)
            M.transpose(bank[1][:, 0:V_ROWS], rows[:, :], g.ident[0:V_ROWS, 0:V_ROWS]).then_inc(small_full, 1)
            pe.wait_ge(d_coup, 16)
            for cm in range(C):
                for cn in range(C):
                    o = D * cm + P * cn
                    last = M.transpose(bank[2][:, o:o + P], coup[:, cn, P * cm:P * cm + P], g.ident[:, :])
            last.then_inc(small_full, 1)
            pe.wait_ge(small_out, 3)
            M.transpose(bank[3][0:1, 0:P], coup_abs[:, :], g.ident[:, :]).then_inc(small_full, 1)
            pe.wait_ge(small_out, 4)
            pe.wait_ge(consts_made, 1)
            M.matmul(bank[0][:, 0:1], ones_row[:, :], coup_top[:, :], start=True, stop=True).then_inc(small_full, 1)
            pe.wait_ge(d_emb, 16)
            for m in range(2 * C):
                for c in range(C):
                    last = M.matmul(bank[1][:, B * m:B * m + B], w_emb[:, c, P * m:P * m + P],
                                    g.condT[:, c, :], start=(c == 0), stop=(c == C - 1))
            last.then_inc(small_full, 1)

            def tiles(src, n, out, full):
                c = n // NB
                for i in range(BB):
                    last = M.transpose(out[:, P * i:P * i + P], src[:, BB * (n % NB) + i, P * c:P * c + P],
                                       g.ident[:, :])
                last.then_inc(full, 1)

            for n in range(2 * NB):
                pe.wait_ge(d_x[n % NB], 16)
                if n >= 2:
                    pe.wait_ge(x_out, n - 1)
                tiles(x_tok, n, bank[4 + n % 2], x_full)
            for n in range(2 * NB):
                pe.wait_ge(xn_ready, BB * (n % NB) + BB)
                if n >= 2:
                    pe.wait_ge(xn_out, n - 1)
                tiles(xn_tok, n, bank[6 + n % 2], xn_full)


def project0(nc, ctx, a, g):
    sb = lambda name, shape, dt=F32: ctx.enter_context(nc.sbuf_tensor(name, shape, dt))
    sem = lambda name: ctx.enter_context(nc.semaphore(name))
    square = sb("square0", [P, 2, 512])
    log_ms = sb("log_ms0", [P, 2, 512])
    rstd = sb("rstd0", [P, 2, 512])
    even = sb("even", [P, 1])
    odd = sb("odd", [P, 1])
    gains = sb("gains", [P, 3])
    raw_full, raw_done = sem("raw_full"), sem("raw_done")
    sq_ready, ms_full, rstd_ready = sem("sq_ready"), sem("ms_full"), sem("rstd_ready0")
    act_chain, dve_chain = sem("act_chain0"), sem("dve_chain0")
    v_full, v_out = sem("v_full"), sem("v_out")
    zeroed = sem("zeroed")
    units = [(w, m, n) for w in range(2) for m in range(C) for n in range(NB)]
    bank = g.bank
    xm = lambda c, n: g.xm[:, c, BB * n:BB * n + BB, :].rearrange("p b t -> p (b t)")

    with nc.Block() as block:
        @block.gpsimd
        def _(pool):
            nc.gpsimd.memset(g.v0[:, :, :, :], 0.0).then_inc(zeroed, 1)

        @block.tensor
        def _(pe):
            M = nc.tensor
            pe.wait_ge(g.d_w0, 32)

            def mean_square(u):
                pe.wait_ge(sq_ready, u + 1)
                if u >= 2:
                    pe.wait_ge(act_chain, u - 1)
                M.matmul(bank[4 + u % 2][:, :], g.block_w[:, :], square[:, u % 2, :], start=True,
                         stop=True).then_inc(ms_full, 1)

            for u, (w, m, n) in enumerate(units):
                if u >= 4:
                    pe.wait_ge(raw_done, u - 3)
                for c in range(C):
                    o = D * w + P * m
                    last = M.matmul(bank[u % 4][:, :], g.w_qkv0[:, c, o:o + P], xm(c, n),
                                    start=(c == 0), stop=(c == C - 1))
                last.then_inc(raw_full, 1)
                if u:
                    mean_square(u - 1)
            mean_square(len(units) - 1)
            for i in range(B // 2):
                if i >= 2:
                    pe.wait_ge(v_out, i - 1)
                for k in range(2):
                    for c in range(C):
                        last = M.matmul(bank[6 + i % 2][:, D * k:D * k + D], g.xm[:, c, 2 * i + k, :],
                                        g.w_qkv0[:, c, 2 * D:3 * D], start=(c == 0), stop=(c == C - 1))
                last.then_inc(v_full, 1)

        @block.scalar
        def _(act):
            A = nc.scalar
            chain = Count(act, act_chain)
            for u in range(len(units) + 1):
                if u < len(units):
                    act.wait_ge(raw_full, u + 1)
                    if u >= 2:
                        act.wait_ge(ms_full, u - 1)
                    A.activation(square[:, u % 2, :], bank[u % 4][:, :], ACT.Square).then_inc(sq_ready, 1)
                if u:
                    v = u - 1
                    act.wait_ge(ms_full, v + 1)
                    n = chain(A.activation(log_ms[:, v % 2, :], bank[4 + v % 2][:, :], ACT.Ln,
                                           bias=g.eps6[:, :]))
                    chain.wait(n)
                    if v >= 2:
                        act.wait_ge(raw_done, v - 1)
                    A.activation(rstd[:, v % 2, :], log_ms[:, v % 2, :], ACT.Exp,
                                 scale=-0.5).then_inc(rstd_ready, 1)
            act.wait_ge(zeroed, 1)
            for i in range(B // 2):
                act.wait_ge(v_full, i + 1)
                src = bank[6 + i % 2][:, :].rearrange("p (b h e) -> p b h e", b=2, e=D0)
                for odd_heads in range(2):
                    dst = g.v0[:, odd_heads, 2 * i:2 * i + 2, :].rearrange("p b (h e) -> p b h e", e=D0)
                    last = A.activation(dst[:, :, odd_heads::2, :], src[:, :, odd_heads::2, :], ACT.Copy)
                last.then_inc(v_out, 1)

        @block.vector
        def _(dve):
            V = nc.vector
            chain = Count(dve, dve_chain)
            heads = g.block_w[:, :].rearrange("p (h e) -> p h e", e=D0)
            n = chain(V.tensor_reduce(even[:, :], heads[:, ::2, 0], op=ADD, axis=AX_X))
            chain.wait(n)
            n = chain(V.tensor_scalar(even[:, :], even[:, :], float(D0), None, MUL))
            chain.wait(n)
            n = chain(V.tensor_scalar(odd[:, :], even[:, :], -1.0, 1.0, MUL, ADD))
            chain.wait(n)
            chain(V.tensor_scalar(gains[:, 0:1], g.vec[:, V_GQ:V_GQ + 1], D0 ** -0.5, None, MUL))
            chain(V.tensor_tensor(gains[:, 1:2], g.vec[:, V_GK:V_GK + 1], even[:, :], MUL))
            n = chain(V.tensor_tensor(gains[:, 2:3], g.vec[:, V_GK:V_GK + 1], odd[:, :], MUL))
            chain.wait(n)
            for u, (w, m, n) in enumerate(units):
                dve.wait_ge(rstd_ready, u + 1)
                outs = [(g.q0, 0)] if w == 0 else [(g.k0[0], 1), (g.k0[1], 2)]
                for t, i in outs:
                    last = V.scalar_tensor_tensor(t[:, m, 512 * n:512 * n + 512], bank[u % 4][:, :],
                                                  gains[:, i:i + 1], rstd[:, u % 2, :], MUL, MUL)
                last.then_inc(raw_done, 1)


def attend0(nc, ctx, a, g):
    sb = lambda name, shape, dt=F32: ctx.enter_context(nc.sbuf_tensor(name, shape, dt))
    sem = lambda name: ctx.enter_context(nc.semaphore(name))
    neg_max = sb("neg_max0", [P, 2, 4])
    sums = sb("sums0", [P, 2, 4])
    inv = sb("inv0", [P, 2, 4])
    prob = sb("prob0", [P, 2, 4, T])
    probT = sb("probT0", [P, 2, 512])
    o0 = g.xm
    w_res = sb("w_res0", [P, C, D])
    s_full, max_ready, p_ready = sem("s_full"), sem("max_ready"), sem("p_ready")
    inv_ready, pn_ready = sem("inv_ready"), sem("pn_ready")
    t_full, t_out, o_full, o_out = sem("t_full"), sem("t_out"), sem("o_full"), sem("o_out")
    w_made, y_full, y_out = sem("w_made"), sem("y_full"), sem("y_out")
    ada_full, drive_ready = sem("ada_full"), sem("drive_ready")
    bias_made, w_copied = sem("bias_made"), sem("w_copied")
    bank = g.bank
    U = B * 4

    with nc.Block() as block:
        @block.tensor
        def _(pe):
            M = nc.tensor
            pe.wait_ge(g.d_ada, 16)
            for m in range(6 * C):
                for c in range(C):
                    last = M.matmul(bank[7][:, B * m:B * m + B], g.ada_w[:, c, P * m:P * m + P],
                                    g.condT[:, c, :], start=(c == 0), stop=(c == C - 1))
            last.then_inc(ada_full, 1)

            def scores(u):
                b, r = divmod(u, 4)
                if u >= 3:
                    pe.wait_ge(p_ready, u - 2)
                rs = slice(32 * r, 32 * r + 32)
                for m in range(C):
                    for e in range(2):
                        o = T * (2 * m + e)
                        last = M.matmul(bank[u % 3][:, o:o + T], g.q0[rs, m, T * b:T * b + T],
                                        g.k0[e][rs, m, T * b:T * b + T], start=True, stop=True)
                last.then_inc(s_full, 1)

            def turn(u):
                pe.wait_ge(pn_ready, u + 1)
                if u >= 2:
                    pe.wait_ge(t_out, u - 1)
                for i in range(4):
                    last = M.transpose(bank[3 + u % 2][:, T * i:T * i + T], prob[:, u % 2, i, :], g.ident[:, :])
                last.then_inc(t_full, 1)

            def weigh(u):
                b, r = divmod(u, 4)
                pe.wait_ge(t_out, u + 1)
                if r == 0 and b >= 2:
                    pe.wait_ge(o_out, b - 1)
                rs = slice(32 * r, 32 * r + 32)
                for m in range(C):
                    for e in range(2):
                        i = 2 * m + e
                        last = M.matmul(bank[5 + b % 2][rs, T * m:T * m + T],
                                        g.v0[:, e, b, P * m + 32 * r:P * m + 32 * r + 32],
                                        probT[:, u % 2, T * i:T * i + T], start=(e == 0), stop=(e == 1))
                last.then_inc(o_full, 1)

            scores(0)
            for u in range(U + 1):
                if u + 1 < U:
                    scores(u + 1)
                if u < U:
                    turn(u)
                if u:
                    weigh(u - 1)
            pe.wait_ge(w_made, C)
            pe.wait_ge(o_out, B)
            for i in range(C * NB):
                m, n = divmod(i, NB)
                if i >= 3:
                    pe.wait_ge(y_out, i - 2)
                for c in range(C):
                    last = M.matmul(bank[i % 3][:, :], w_res[:, c, P * m:P * m + P],
                                    o0[:, c, BB * n:BB * n + BB, :].rearrange("p b t -> p (b t)"),
                                    start=(c == 0), stop=(c == C - 1))
                last.then_inc(y_full, 1)

        @block.vector
        def _(dve):
            V = nc.vector
            for c in range(C):
                ws = w_res[:, c, :]
                V.tensor_copy(ws, g.w_out0[:, c, :]).then_inc(w_copied, 1)
                dve.wait_ge(w_copied, c + 1)
                sl = slice(P * c, P * c + P)
                V.tensor_tensor(w_res[:, c, sl], g.w_out0[:, c, sl], g.ident[:, :], ADD).then_inc(w_made, 1)
            dve.wait_ge(ada_full, 1)
            for m in range(6 * C):
                one = 1.0 if m // C in (1, 4) else 0.0
                V.tensor_scalar(g.ada[:, m, :], bank[7][:, B * m:B * m + B],
                                g.vec[:, V_ADAB + m:V_ADAB + m + 1], one, ADD, ADD)

            def top(u):
                dve.wait_ge(s_full, u + 1)
                if u >= 2:
                    dve.wait_ge(p_ready, u - 1)
                V.tensor_reduce(neg_max[:, u % 2, :], bank[u % 3][:, :].rearrange("p (h k) -> p h k", h=4),
                                op=ALU.max, axis=AX_X, negate=True).then_inc(max_ready, 1)

            top(0)
            for u in range(U):
                if u + 1 < U:
                    top(u + 1)
                dve.wait_ge(p_ready, u + 1)
                if u >= 2:
                    dve.wait_ge(pn_ready, u - 1)
                V.reciprocal(inv[:, u % 2, :], sums[:, u % 2, :]).then_inc(inv_ready, 1)
                if u:
                    v = u - 1
                    dve.wait_ge(t_full, v + 1)
                    if v >= 2:
                        dve.wait_ge(o_full, v - 1)
                    V.tensor_copy(probT[:, v % 2, :], bank[3 + v % 2][:, :]).then_inc(t_out, 1)
            dve.wait_ge(t_full, U)
            V.tensor_copy(probT[:, (U - 1) % 2, :], bank[3 + (U - 1) % 2][:, :]).then_inc(t_out, 1)
            for i in range(C * NB):
                m, n = divmod(i, NB)
                bs = slice(BB * n, BB * n + BB)
                dve.wait_ge(y_full, i + 1)
                V.tensor_tensor(g.x1[:, :, m, bs].rearrange("p t b -> p b t"),
                                bank[i % 3][:, :].rearrange("p (b t) -> p b t", b=BB),
                                g.xT[:, m, bs, :], ADD).then_inc(y_out, 1)

        @block.scalar
        def _(act):
            A = nc.scalar

            def out(b):
                act.wait_ge(o_full, 4 * b + 4)
                A.activation(o0[:, :, b, :], bank[5 + b % 2][:, 0:C * T].rearrange("p (c t) -> p c t", c=C),
                             ACT.Copy).then_inc(o_out, 1)

            for u in range(U):
                act.wait_ge(max_ready, u + 1)
                if u >= 2:
                    act.wait_ge(t_full, u - 1)
                    act.wait_ge(inv_ready, u - 1)
                for i in range(4):
                    last = A.activation(prob[:, u % 2, i, :], bank[u % 3][:, T * i:T * i + T], ACT.Exp,
                                        bias=neg_max[:, u % 2, i:i + 1], accum_out=sums[:, u % 2, i:i + 1])
                last.then_inc(p_ready, 1)
                if u % 4 == 3 and u > 4:
                    out(u // 4 - 1)
            out(B - 1)
            act.wait_ge(bias_made, 1)
            for m in range(C):
                act.wait_ge(y_out, NB * (m + 1))
                A.activation(g.drive[:, 0:T, m, :], g.x1[:, :, m, :], ACT.Identity,
                             bias=g.drive_b[:, m:m + 1], scale=DT / 2)

        @block.gpsimd
        def _(pool):
            G = nc.gpsimd
            G.tensor_scalar(g.drive_b[:, :], g.vec[:, V_BIAS1:V_BIAS1 + C], DT / 2,
                            -ALPHA / BETA * DT / 2, MUL, ADD).then_inc(bias_made, 1)
            for u in range(U):
                pool.wait_ge(inv_ready, u + 1)
                G.tensor_tensor(prob[:, u % 2, :, :], prob[:, u % 2, :, :],
                                inv[:, u % 2, :].unsqueeze(2).broadcast_to([P, 4, T]), MUL).then_inc(pn_ready, 1)


def scan1(nc, ctx, a, g):
    sb = lambda name, shape, dt=F32: ctx.enter_context(nc.sbuf_tensor(name, shape, dt))
    sem = lambda name: ctx.enter_context(nc.semaphore(name))
    tile = lambda name: sb(name, [P, W1])[:, :]
    y, s2, s3, s4 = tile("s1_y"), tile("s1_s2"), tile("s1_s3"), tile("s1_s4")
    sq, cube, rest = tile("s1_sq"), tile("s1_cube"), tile("s1_rest")
    p_raw, p1, p2, p3, p4 = (tile(f"s1_p{i}") for i in range(5))
    m1, m2, m3, m4 = (tile(f"s1_m{i}") for i in range(1, 5))
    qd1, qd2, qd3, gmq = tile("s1_qd1"), tile("s1_qd2"), tile("s1_qd3"), tile("s1_gmq")
    base1, base2, base3, base4 = (tile(f"s1_base{i}") for i in range(1, 5))
    acc2, acc3, acc4, acc5 = (tile(f"s1_acc{i}") for i in range(2, 6))
    msum, msum2, msum3, mscaled, pm = (tile(f"s1_ms{i}") for i in range(5))
    th_f = tile("s1_tanh")
    warm = sb("s1_warm", [P, 1])
    th_hi = sb("s1_tanh_hi", [P, W1], F16)
    th_lo = sb("s1_tanh_lo", [P, W1], F16)
    coupled = g.bank[0][:, 0:W1]
    s_ready = sem("s_ready")
    hi_ready, th_ready, lo_ready = sem("hi_ready"), sem("th_ready"), sem("lo_ready")
    coupled_ready = sem("coupled_ready")
    dve_done, pool_done = sem("dve_done"), sem("pool_done")
    lap_done, lap_go = sem("lap_done"), sem("lap_go")
    init, last_out, x2_done = sem("init1"), sem("last_out"), sem("x2_done")
    ND, NP = 31, 8
    MSUM_AT = 19
    h = DT / 2
    laps = T // LAP
    trace = g.trace[:, :, :, :].rearrange("p t c b -> p (t c b)")
    drive = g.drive[:, :, :, :].rearrange("p t c b -> p (t c b)")

    def end_lap(eng, lap):
        eng.sem_inc(lap_done, 1)
        eng.wait_ge(lap_go, lap + 1)

    with nc.Block() as block:
        @block.sync
        def _(sp):
            with sp.Fori(0, laps) as lap:
                sp.wait_ge(lap_done, lap * 4 + 4)
                for s, n in ((s_ready, 4), (hi_ready, 4), (th_ready, 4), (lo_ready, 4),
                             (coupled_ready, 4), (dve_done, ND), (pool_done, NP)):
                    sp.sem_inc(s, -n * LAP)
                sp.sem_inc(lap_go, 1)

        @block.vector
        def _(dve):
            V = nc.vector
            STT = V.scalar_tensor_tensor
            V.tensor_copy(y, g.condT[:, :, :].rearrange("p c b -> p (c b)")).then_inc(init, 1)
            V.tensor_scalar(p_raw, g.condT[:, :, :].rearrange("p c b -> p (c b)"), -ALPHA / BETA,
                            None, ADD).then_inc(init, 1)
            dve.wait_ge(init, 2)
            dve.sem_inc(s_ready, 1)
            with dve.Fori(0, laps) as lap:
                for j in range(LAP):
                    done = [ND * j]

                    def do(ins):
                        ins.then_inc(dve_done, 1)
                        done[0] += 1
                        return done[0]

                    def after(n):
                        dve.wait_ge(dve_done, n)

                    def low(stage):
                        dve.wait_ge(th_ready, 4 * j + stage)
                        V.tensor_tensor(th_lo[:, :], th_f, th_hi[:, :], SUB).then_inc(lo_ready, 1)

                    def advance(stage, out, scale, n):
                        dve.wait_ge(coupled_ready, 4 * j + stage)
                        after(n)
                        STT(out, coupled, g.coup_scale[:, scale:scale + 1], rest, MUL, ADD).then_inc(s_ready, 1)

                    def stage_input(stage):
                        dve.wait_ge(s_ready, 4 * j + stage)

                    q = trace[:, bass.ds(lap * (LAP * W1) + W1 * j, W1)]
                    gh = drive[:, bass.ds(lap * (LAP * W1) + W1 * j, W1)]
                    n = do(V.tensor_scalar(p1, p_raw, CLAMP - ALPHA / BETA, -CLAMP - ALPHA / BETA, ALU.min, ALU.max))
                    stage_input(1)
                    nq = do(V.tensor_scalar(q, y, CLAMP, -CLAMP, ALU.min, ALU.max))
                    after(n)
                    n = do(STT(pm, p1, -h, gh, MUL, ADD))
                    after(nq)
                    ns = do(V.tensor_tensor(sq, q, q, MUL))
                    nm = do(STT(m1, p1, -BETA, q, MUL, ADD))
                    after(ns)
                    nc_ = do(STT(cube, sq, -3.0, q, ADD, MUL))
                    nb = do(V.tensor_tensor(base1, pm, q, ADD))
                    low(1)
                    after(nb)
                    nr = do(STT(rest, cube, -h / 3, base1, MUL, ADD))
                    n = do(STT(p2, m1, h * EPSILON, p1, MUL, ADD))
                    after(n)
                    dve.wait_ge(pool_done, NP * j + 3)
                    do(STT(base2, p2, -h, qd1, MUL, ADD))
                    advance(1, s2, 0, nr)
                    stage_input(2)
                    ns = do(V.tensor_tensor(sq, s2, s2, MUL))
                    nm = do(STT(m2, p2, -BETA, s2, MUL, ADD))
                    after(ns)
                    nc_ = do(STT(cube, sq, -3.0, s2, ADD, MUL))
                    low(2)
                    after(nm)
                    n = do(STT(p3, m2, h * EPSILON, p1, MUL, ADD))
                    after(nc_)
                    nr = do(STT(rest, cube, -h / 3, base2, MUL, ADD))
                    after(n)
                    do(STT(base3, p3, -DT, qd2, MUL, ADD))
                    do(V.tensor_tensor(acc2, gmq, s2, ADD))
                    advance(2, s3, 0, nr)
                    stage_input(3)
                    ns = do(V.tensor_tensor(sq, s3, s3, MUL))
                    nm = do(STT(m3, p3, -BETA, s3, MUL, ADD))
                    assert nm == ND * j + MSUM_AT
                    after(ns)
                    nc_ = do(STT(cube, sq, -3.0, s3, ADD, MUL))
                    low(3)
                    n = do(STT(acc3, s3, 2.0, acc2, MUL, ADD))
                    after(nc_)
                    nr = do(STT(rest, cube, -DT / 3, base3, MUL, ADD))
                    n4 = do(STT(p4, m3, DT * EPSILON, p1, MUL, ADD))
                    after(n4)
                    do(STT(acc4, p4, -h, acc3, MUL, ADD))
                    advance(3, s4, 1, nr)
                    stage_input(4)
                    ns = do(V.tensor_tensor(sq, s4, s4, MUL))
                    nz = do(V.tensor_tensor(acc5, acc4, s4, ADD))
                    after(ns)
                    nc_ = do(STT(cube, sq, -3.0, s4, ADD, MUL))
                    low(4)
                    after(nz)
                    nz = do(V.tensor_scalar(base4, acc5, 1 / 3, None, MUL))
                    nm = do(STT(m4, p4, -BETA, s4, MUL, ADD))
                    after(nz)
                    nr = do(STT(rest, cube, -DT / 18, base4, MUL, ADD))
                    after(nm)
                    dve.wait_ge(pool_done, NP * j + NP)
                    n = do(STT(p_raw, m4, DT * EPSILON / 6, mscaled, MUL, ADD))
                    advance(4, y, 2, n)
                    assert done[0] == ND * j + ND, done[0]
                dve.wait_ge(s_ready, 4 * LAP + 1)
                end_lap(dve, lap)
            dve.wait_ge(s_ready, 1)
            V.tensor_scalar(trace[:, T * W1:], y, CLAMP, -CLAMP, ALU.min, ALU.max).then_inc(last_out, 1)
            dve.wait_ge(last_out, 1)
            for c in range(C):
                V.tensor_tensor(g.x2[:, c, :, :], g.x1[:, :, c, :].rearrange("p t b -> p b t"),
                                g.trace[:, 1:T + 1, c, :].rearrange("p t b -> p b t"), ADD)

        @block.gpsimd
        def _(pool):
            G = nc.gpsimd
            with pool.Fori(0, laps) as lap:
                for j in range(LAP):
                    q = trace[:, bass.ds(lap * (LAP * W1) + W1 * j, W1)]
                    gh = drive[:, bass.ds(lap * (LAP * W1) + W1 * j, W1)]
                    done = [NP * j]

                    def do(ins, wait=True):
                        ins.then_inc(pool_done, 1)
                        done[0] += 1
                        if wait:
                            pool.wait_ge(pool_done, done[0])

                    pool.wait_ge(dve_done, ND * j + 2)
                    do(G.tensor_tensor(qd1, gh, q, ADD))
                    do(G.tensor_tensor(qd2, qd1, gh, ADD), False)
                    do(G.tensor_tensor(gmq, gh, q, SUB), False)
                    pool.wait_ge(dve_done, ND * j + MSUM_AT)
                    do(G.tensor_tensor(msum, m2, m3, ADD))
                    do(G.tensor_tensor(msum2, msum, msum, ADD))
                    do(G.tensor_tensor(msum3, msum2, m1, ADD))
                    do(G.tensor_scalar(qd3, msum3, DT * EPSILON / 6, None, MUL))
                    do(G.tensor_tensor(mscaled, qd3, p1, ADD), False)
                end_lap(pool, lap)

        @block.scalar
        def _(act):
            A = nc.scalar
            A.activation(warm[:, :], g.eps6[:, :], ACT.Tanh)
            with act.Fori(0, laps) as lap:
                for j in range(LAP):
                    for i, s in enumerate((y, s2, s3, s4)):
                        act.wait_ge(s_ready, 4 * j + i + 1)
                        A.activation(th_hi[:, :], s, ACT.Tanh).then_inc(hi_ready, 1)
                        A.activation(th_f, s, ACT.Tanh).then_inc(th_ready, 1)
                end_lap(act, lap)

        @block.tensor
        def _(pe):
            def product(w, th, first, last):
                for c in range(C):
                    for m in range(C):
                        o = D * c + P * m
                        ins = nc.tensor.matmul(coupled[:, B * m:B * m + B], w[:, o:o + P],
                                               th[:, B * c:B * c + B], start=(first and c == 0 and m == 0),
                                               stop=(last and c == C - 1), skip_group_check=True)
                return ins

            with pe.Fori(0, laps) as lap:
                for i in range(4 * LAP):
                    pe.wait_ge(hi_ready, i + 1)
                    product(g.coup_hi, th_hi, True, False)
                    product(g.coup_lo, th_hi, False, False)
                    pe.wait_ge(lo_ready, i + 1)
                    product(g.coup_hi, th_lo, False, True).then_inc(coupled_ready, 1)
                end_lap(pe, lap)


def norm_split(nc, ctx, a, g, tag, scale, shift, xh, xl, loads):
    sb = lambda name, shape, dt=F32: ctx.enter_context(nc.sbuf_tensor(name + tag, shape, dt))
    sem = lambda name: ctx.enter_context(nc.semaphore(name + tag))
    xc = sb("centred", [P, C, 2, 512])
    square = sb("square", [P, C, 2, 512])
    log_var = sb("log_var", [P, 2, 512])
    rstd = sb("rstd", [P, 2, 512])
    mod = sb("modulated", [P, C, 2, 512])
    mean_full, xc_ready, sq_ready, var_full = sem("mean_full"), sem("xc_ready"), sem("sq_ready"), sem("var_full")
    log_ready, rstd_ready, xhat_ready = sem("log_ready"), sem("rstd_ready"), sem("xhat_ready")
    mod_ready, hi_ready, lo_ready = sem("mod_ready"), sem("hi_ready"), sem("lo_ready")
    bank = g.bank
    x2 = g.x2[:, :, :, :].rearrange("p c b t -> p c (b t)")
    blk = lambda n: slice(512 * n, 512 * n + 512)

    with nc.Block() as block:
        @block.sync
        def _(sp):
            loads(sp)

        @block.tensor
        def _(pe):
            M = nc.tensor
            for n in range(NB):
                for c in range(C):
                    last = M.matmul(bank[n][:, :], g.mean_w[:, :], x2[:, c, blk(n)], start=(c == 0),
                                    stop=(c == C - 1))
                last.then_inc(mean_full, 1)
            for n in range(NB):
                pe.wait_ge(sq_ready, C * n + C)
                for c in range(C):
                    last = M.matmul(bank[4 + n][:, :], g.mean_w[:, :], square[:, c, n % 2, :],
                                    start=(c == 0), stop=(c == C - 1))
                last.then_inc(var_full, 1)

        @block.vector
        def _(dve):
            V = nc.vector

            def centre(n):
                dve.wait_ge(mean_full, n + 1)
                for c in range(C):
                    if n >= 2:
                        dve.wait_ge(mod_ready, C * (n - 2) + c + 1)
                    V.tensor_tensor(xc[:, c, n % 2, :], x2[:, c, blk(n)], bank[n][:, :],
                                    SUB).then_inc(xc_ready, 1)

            centre(0)
            for n in range(NB):
                if n + 1 < NB:
                    centre(n + 1)
                dve.wait_ge(rstd_ready, n + 1)
                dve.wait_ge(sq_ready, C * n + C)
                for c in range(C):
                    V.tensor_tensor(xc[:, c, n % 2, :], xc[:, c, n % 2, :], rstd[:, n % 2, :],
                                    MUL).then_inc(xhat_ready, 1)
                for c in range(C):
                    dve.wait_ge(xhat_ready, C * n + c + 1)
                    if n >= 2:
                        dve.wait_ge(hi_ready, C * (n - 2) + c + 1)
                    for i in range(BB):
                        b = BB * n + i
                        last = V.tensor_scalar(mod[:, c, n % 2, T * i:T * i + T], xc[:, c, n % 2, T * i:T * i + T],
                                               g.ada[:, C * scale + c, b:b + 1],
                                               g.ada[:, C * shift + c, b:b + 1], MUL, ADD)
                    last.then_inc(mod_ready, 1)
                for c in range(C):
                    dve.wait_ge(hi_ready, C * n + c + 1)
                    V.tensor_tensor(xl[:, c, blk(n)], mod[:, c, n % 2, :], xh[:, c, blk(n)].bitcast(F32),
                                    SUB).then_inc(lo_ready, 1)

        @block.scalar
        def _(act):
            A = nc.scalar
            for n in range(NB + 1):
                if n < NB:
                    for c in range(C):
                        act.wait_ge(xc_ready, C * n + c + 1)
                        if n >= 2:
                            act.wait_ge(var_full, n - 1)
                        A.activation(square[:, c, n % 2, :], xc[:, c, n % 2, :], ACT.Square).then_inc(sq_ready, 1)
                    act.wait_ge(var_full, n + 1)
                    A.activation(log_var[:, n % 2, :], bank[4 + n][:, :], ACT.Ln, bias=g.eps6[:, :]).then_inc(log_ready, 1)
                    act.wait_ge(log_ready, n + 1)
                    if n >= 2:
                        act.wait_ge(xhat_ready, C * (n - 1))
                    A.activation(rstd[:, n % 2, :], log_var[:, n % 2, :], ACT.Exp, scale=-0.5).then_inc(rstd_ready, 1)
                if n:
                    for c in range(C):
                        act.wait_ge(mod_ready, C * (n - 1) + c + 1)
                        if n >= 3:
                            act.wait_ge(lo_ready, C * (n - 3) + c + 1)
                        A.activation(xh[:, c, blk(n - 1)], mod[:, c, (n - 1) % 2, :], ACT.Copy).then_inc(hi_ready, 1)


def attend2(nc, ctx, a, g, xh, xl):
    sb = lambda name, shape, dt=F32: ctx.enter_context(nc.sbuf_tensor(name, shape, dt))
    sem = lambda name: ctx.enter_context(nc.semaphore(name))
    HG, UNITS, GROUPS, INNER = 4, 16, 64, H2 * D2
    w_h = sb("w2_hi", [P, 3, C, 512], F32R)
    w_l = sb("w2_lo", [P, 3, C, 512], F32R)
    w_stage = g.w_stage
    ow_stage = g.ow_stage
    ow_h = sb("ow_hi", [P, HG, D], F32R)
    ow_l = sb("ow_lo", [P, HG, D], F32R)
    o_h = sb("o2_hi", [P, 2, HG, 512], F32R)
    o_l = sb("o2_lo", [P, 2, HG, 512], F32R)
    q2 = sb("q2", [P, 2, HG, 512])
    k2 = sb("k2", [P, 2, HG, 512])
    v2 = sb("v2", [P, 2, BB, 512])
    prob = sb("prob2", [P, 2, HG, T])
    probT = sb("probT2", [P, 2, 512])
    neg_max = sb("neg_max2", [P, 2, HG])
    sums = sb("sums2", [P, 2, HG])
    inv = sb("inv2", [P, 2, HG])
    q_bias = sb("q_bias", [P, H2])
    gate_b = sb("gate_b", [P, C, B])
    wh_ready, wl_ready = sem("wh_ready"), sem("wl_ready")
    owh_ready, owl_ready = sem("owh_ready"), sem("owl_ready")
    proj_full, q_out, kv_out = sem("proj_full"), sem("q_out"), sem("kv_out")
    s_full, max_ready, p_ready, inv_ready, pn_ready = (
        sem("s_full2"), sem("max_ready2"), sem("p_ready2"), sem("inv_ready2"), sem("pn_ready2"))
    t_full, t_out, o_full, oh_ready, ol_ready = (
        sem("t_full2"), sem("t_out2"), sem("o_full2"), sem("oh_ready2"), sem("ol_ready2"))
    y_full, y_out = sem("y_full2"), sem("y_out2")
    small_made, base_made = sem("small_made2"), sem("base_made2")
    bank = g.bank
    STEPS = 12
    evac_steps = {}

    def proj_evacuated(eng, i):
        u, s = divmod(i, STEPS)
        if s < 4:
            eng.wait_ge(q_out, 4 * u + s + 1)
        else:
            eng.wait_ge(kv_out, 8 * u + s - 3)

    def slots():
        for p in range(UNITS + 2):
            for k in range(4):
                yield p, k, 4 * (p - 1) + k

    with nc.Block() as block:
        @block.sync
        def _(sp):
            for hg in range(1, HG):
                sp.wait_ge(wl_ready, 3 * hg)
                load_w2(sp, a, g, hg)
                sp.wait_ge(owl_ready, hg)
                load_ow(sp, a, g, hg)
                if hg >= 2:
                    sp.wait_ge(kv_out, 8 * 4 * (hg - 1))
                load_vb(sp, a, g, hg)

        @block.tensor
        def _(pe):
            M = nc.tensor

            def three(out, parts, last_of):
                n = 0
                for sh, sl, mh, ml in parts:
                    for s, m in ((sh, mh), (sh, ml), (sl, mh)):
                        ins = M.matmul(out, s, m, start=(n == 0), stop=(n == 3 * len(parts) - 1))
                        n += 1
                ins.then_inc(last_of, 1)

            def project(i):
                u, s = divmod(i, STEPS)
                hg, bg = divmod(u, 4)
                w, j = divmod(s, 4)
                pe.wait_ge(wl_ready, 3 * hg + w + 1)
                if i >= 2:
                    proj_evacuated(pe, i - 2)
                parts = []
                for c in range(C):
                    if w < 2:
                        cols, toks = slice(D2 * j, D2 * j + D2), slice(512 * bg, 512 * bg + 512)
                        parts.append((w_h[:, w, c, cols], w_l[:, w, c, cols], xh[:, c, toks], xl[:, c, toks]))
                    else:
                        t0 = 512 * bg + T * j
                        parts.append((xh[:, c, t0:t0 + T], xl[:, c, t0:t0 + T], w_h[:, w, c, :], w_l[:, w, c, :]))
                three(bank[i % 2][:, :], parts, proj_full)

            for p, k, grp in slots():
                if 0 <= grp < GROUPS:
                    u = p - 1
                    pe.wait_ge(q_out, 4 * u + 4)
                    pe.wait_ge(kv_out, 8 * u + 4)
                    if grp >= 2:
                        pe.wait_ge(p_ready, grp - 1)
                    ts = slice(T * k, T * k + T)
                    for h in range(HG):
                        last = M.matmul(bank[2 + grp % 2][:, T * h:T * h + T], q2[:, u % 2, h, ts],
                                        k2[:, u % 2, h, ts], start=True, stop=True)
                    last.then_inc(s_full, 1)
                i = STEPS * p + 3 * k
                if p < UNITS:
                    project(i)
                if 0 <= grp - 1 < GROUPS:
                    v = grp - 1
                    pe.wait_ge(pn_ready, v + 1)
                    if v >= 2:
                        pe.wait_ge(t_out, v - 1)
                    for h in range(HG):
                        last = M.transpose(bank[4 + v % 2][:, T * h:T * h + T], prob[:, v % 2, h, :], g.ident[:, :])
                    last.then_inc(t_full, 1)
                if p < UNITS:
                    project(i + 1)
                if 0 <= grp - 2 < GROUPS:
                    v = grp - 2
                    u, b = divmod(v, 4)
                    pe.wait_ge(kv_out, 8 * u + 8)
                    pe.wait_ge(t_out, v + 1)
                    pe.wait_ge(ol_ready, v)
                    for h in range(HG):
                        last = M.matmul(bank[6][:, T * h:T * h + T], v2[:, u % 2, b, D2 * h:D2 * h + D2],
                                        probT[:, v % 2, T * h:T * h + T], start=True, stop=True)
                    last.then_inc(o_full, 1)
                if p < UNITS:
                    project(i + 2)
                if p >= 2 and k >= 2:
                    u, m = p - 2, k - 2
                    pe.wait_ge(ol_ready, 4 * u + 4)
                    pe.wait_ge(owl_ready, u // 4 + 1)
                    if 2 * u + m:
                        pe.wait_ge(y_out, 2 * u + m)
                    ms = slice(P * m, P * m + P)
                    three(bank[7][:, :], [(ow_h[:, h, ms], ow_l[:, h, ms], o_h[:, u % 2, h, :],
                                           o_l[:, u % 2, h, :]) for h in range(HG)], y_full)

        def conversions(p, k):
            if p % 4 == 3 and p < UNITS - 1 and k >= 2:
                yield "w", p // 4 + 1, k - 2
            if p % 4 == 0 and 4 <= p < UNITS and k == 0:
                yield "w", p // 4, 2
            if p % 4 == 2 and 6 <= p < UNITS and k == 0:
                yield "ow", p // 4, 0

        first = [("w", 0, 0), ("w", 0, 1), ("w", 0, 2), ("ow", 0, 0)]

        @block.scalar
        def _(act):
            A = nc.scalar

            def convert(what, hg, part):
                if what == "w":
                    act.wait_ge(g.d_w2, 48 * (hg + 1))
                    if hg:
                        act.wait_ge(proj_full, STEPS * (4 * hg - 1) + 4 * part + 4)
                    for c in range(C):
                        A.activation(w_h[:, part, c, :], w_stage[:, part, c, :], ACT.Copy).then_inc(wh_ready, 1)
                else:
                    act.wait_ge(g.d_ow, 16 * (hg + 1))
                    if hg:
                        act.wait_ge(y_full, 2 * 4 * hg)
                    for c in range(2):
                        A.activation(ow_h[:, 2 * c:2 * c + 2, :], ow_stage[:, 2 * c:2 * c + 2, :],
                                     ACT.Copy).then_inc(owh_ready, 1)

            for item in first:
                convert(*item)
            act.wait_ge(small_made, 1)
            for p, k, grp in slots():
                for item in conversions(p, k):
                    convert(*item)
                if 0 <= grp < GROUPS:
                    act.wait_ge(max_ready, grp + 1)
                    if grp >= 2:
                        act.wait_ge(t_full, grp - 1)
                        act.wait_ge(inv_ready, grp - 1)
                    for h in range(HG):
                        last = A.activation(prob[:, grp % 2, h, :], bank[2 + grp % 2][:, T * h:T * h + T], ACT.Exp,
                                            bias=neg_max[:, grp % 2, h:h + 1], accum_out=sums[:, grp % 2, h:h + 1])
                    last.then_inc(p_ready, 1)
                for i in range(STEPS * p + 3 * k, STEPS * p + 3 * k + 3):
                    u, s = divmod(i, STEPS)
                    if p < UNITS and s < 4:
                        act.wait_ge(proj_full, i + 1)
                        if u >= 2:
                            act.wait_ge(s_full, 4 * (u - 1))
                        h = HG * (u // 4) + s
                        A.activation(q2[:, u % 2, s, :], bank[i % 2][:, :], ACT.Identity,
                                     bias=q_bias[:, h:h + 1], scale=D2 ** -0.5).then_inc(q_out, 1)
                if 0 <= grp - 2 < GROUPS:
                    v = grp - 2
                    u, b = divmod(v, 4)
                    act.wait_ge(o_full, v + 1)
                    if u >= 2:
                        act.wait_ge(y_full, 2 * (u - 1))
                    A.activation(o_h[:, u % 2, :, T * b:T * b + T],
                                 bank[6][:, :].rearrange("p (h t) -> p h t", h=HG), ACT.Copy).then_inc(oh_ready, 1)

        @block.vector
        def _(dve):
            V = nc.vector

            def convert(what, hg, part):
                if what == "w":
                    for c in range(C):
                        dve.wait_ge(wh_ready, C * (3 * hg + part) + c + 1)
                        last = V.tensor_tensor(w_l[:, part, c, :], w_stage[:, part, c, :],
                                               w_h[:, part, c, :].bitcast(F32), SUB)
                    last.then_inc(wl_ready, 1)
                else:
                    for c in range(2):
                        dve.wait_ge(owh_ready, 2 * hg + c + 1)
                        hs = slice(2 * c, 2 * c + 2)
                        last = V.tensor_tensor(ow_l[:, hs, :], ow_stage[:, hs, :], ow_h[:, hs, :].bitcast(F32), SUB)
                    last.then_inc(owl_ready, 1)

            V.tensor_scalar(q_bias[:, :], g.vec[:, V_QKB:V_QKB + H2], D2 ** -0.5, None, MUL).then_inc(small_made, 1)
            for item in first:
                convert(*item)
            for p, k, grp in slots():
                for item in conversions(p, k):
                    convert(*item)
                if 0 <= grp < GROUPS:
                    dve.wait_ge(s_full, grp + 1)
                    if grp >= 2:
                        dve.wait_ge(p_ready, grp - 1)
                    V.tensor_reduce(neg_max[:, grp % 2, :], bank[2 + grp % 2][:, :].rearrange("p (h k) -> p h k", h=HG),
                                    op=ALU.max, axis=AX_X, negate=True).then_inc(max_ready, 1)

                def out(i):
                    u, s = divmod(i, STEPS)
                    if p >= UNITS or s < 4:
                        return
                    dve.wait_ge(proj_full, i + 1)
                    if s < 8:
                        if u >= 2:
                            dve.wait_ge(s_full, 4 * (u - 1))
                        bias = g.vec[:, V_QKB + H2 + HG * (u // 4) + s - 4:][:, 0:1]
                        V.tensor_scalar(k2[:, u % 2, s - 4, :], bank[i % 2][:, :], bias, None, ADD).then_inc(kv_out, 1)
                    else:
                        dve.wait_ge(g.d_vb[u // 4], 16)
                        if u >= 2:
                            dve.wait_ge(o_full, 4 * (u - 1))
                        V.tensor_tensor(v2[:, u % 2, s - 8, :], bank[i % 2][:, :], g.v_bias[:, (u // 4) % 2, :],
                                        ADD).then_inc(kv_out, 1)

                out(STEPS * p + 3 * k)
                if 0 <= grp - 1 < GROUPS:
                    v = grp - 1
                    dve.wait_ge(t_full, v + 1)
                    if v >= 2:
                        dve.wait_ge(o_full, v - 1)
                    V.tensor_copy(probT[:, v % 2, :], bank[4 + v % 2][:, :]).then_inc(t_out, 1)
                if 0 <= grp < GROUPS:
                    dve.wait_ge(p_ready, grp + 1)
                    if grp >= 2:
                        dve.wait_ge(pn_ready, grp - 1)
                    V.reciprocal(inv[:, grp % 2, :], sums[:, grp % 2, :]).then_inc(inv_ready, 1)
                out(STEPS * p + 3 * k + 1)
                if 0 <= grp - 2 < GROUPS:
                    v = grp - 2
                    u, b = divmod(v, 4)
                    dve.wait_ge(oh_ready, v + 1)
                    V.tensor_tensor(o_l[:, u % 2, :, T * b:T * b + T],
                                    bank[6][:, :].rearrange("p (h t) -> p h t", h=HG),
                                    o_h[:, u % 2, :, T * b:T * b + T].bitcast(F32), SUB).then_inc(ol_ready, 1)
                out(STEPS * p + 3 * k + 2)
                if p >= 2 and k >= 2:
                    u, m = p - 2, k - 2
                    dve.wait_ge(y_full, 2 * u + m + 1)
                    dve.wait_ge(base_made, C)
                    if u >= 4:
                        dve.wait_ge(y_out, 2 * (u - 4) + m + 1)
                    for i in range(BB):
                        b = BB * (u % 4) + i
                        last = V.scalar_tensor_tensor(g.x2[:, m, b, :], bank[7][:, T * i:T * i + T],
                                                      g.ada[:, 2 * C + m, b:b + 1], g.x2[:, m, b, :], MUL, ADD)
                    last.then_inc(y_out, 1)

        @block.gpsimd
        def _(pool):
            G = nc.gpsimd
            for c in range(C):
                G.tensor_scalar(gate_b[:, c, :], g.ada[:, 2 * C + c, :], g.vec[:, V_OUTB + c:V_OUTB + c + 1],
                                None, MUL).then_inc(small_made, 1)
            pool.wait_ge(small_made, 1 + C)
            for c in range(C):
                G.tensor_tensor(g.x2[:, c, :, :], g.x2[:, c, :, :],
                                gate_b[:, c, :].unsqueeze(2).broadcast_to([P, B, T]), ADD).then_inc(base_made, 1)
            for grp in range(GROUPS):
                pool.wait_ge(inv_ready, grp + 1)
                G.tensor_tensor(prob[:, grp % 2, :, :], prob[:, grp % 2, :, :],
                                inv[:, grp % 2, :].unsqueeze(2).broadcast_to([P, HG, T]), MUL).then_inc(pn_ready, 1)


def load_w2(sp, a, g, hg):
    w = a["L2_cond_qkv_w"].rearrange("(c p) n -> p c n", p=P)
    for part in range(3):
        o = H2 * D2 * part + 512 * hg
        sp.dma_start(g.w_stage[:, part, :, :], w[:, :, o:o + 512]).then_inc(g.d_w2, 16)


def load_ow(sp, a, g, hg):
    w = a["L2_cond_out_w"][512 * hg:512 * hg + 512, :].rearrange("(h p) n -> p h n", p=P)
    sp.dma_start(g.ow_stage[:, :, :], w).then_inc(g.d_ow, 16)


def load_vb(sp, a, g, hg):
    o = 2 * H2 * D2 + 512 * hg
    sp.dma_start(g.v_bias[:, hg % 2, :], a["L2_cond_qkv_b"][o:o + 512].partition_broadcast(P)).then_inc(g.d_vb[hg], 16)


def feed_forward(nc, ctx, a, g, xh, xl, x3_dram):
    sb = lambda name, shape, dt=F32: ctx.enter_context(nc.sbuf_tensor(name, shape, dt))
    sem = lambda name: ctx.enter_context(nc.semaphore(name))
    M1 = FF // P
    w1_h, w1_l = sb("w1_hi", [P, C, FF], F32R), sb("w1_lo", [P, C, FF], F32R)
    w2_h, w2_l = sb("ffw2_hi", [P, M1, D], F32R), sb("ffw2_lo", [P, M1, D], F32R)
    act_f = sb("gelu", [P, 2, 512])
    h_h, h_l = sb("hidden_hi", [P, M1, 512], F32R), sb("hidden_lo", [P, M1, 512], F32R)
    x3_tok = sb("x3_tok", [P, 2, 2, D])
    wh_ready, wl_ready = sem("ffwh_ready"), sem("ffwl_ready")
    f_full, gelu_ready, hh_ready, hl_ready = sem("f_full"), sem("gelu_ready"), sem("hh_ready"), sem("hl_ready")
    y_full, y_out, with_b = sem("fy_full"), sem("fy_out"), sem("with_b")
    t_full, t_out = sem("x3t_full"), sem("x3t_out")
    gate_b, gb_made = sb("gate_b2", [P, C, B]), sem("gb_made")
    doubled = sem("doubled")
    bank = g.bank
    pieces = [(g.w1_stage[:, c, o:o + 512], w1_h[:, c, o:o + 512], w1_l[:, c, o:o + 512])
              for o in (0, 512) for c in range(C)]
    pieces += [(g.ffw2_stage[:, k:k + 2, :], w2_h[:, k:k + 2, :], w2_l[:, k:k + 2, :]) for k in range(0, M1, 2)]

    with nc.Block() as block:
        @block.tensor
        def _(pe):
            M = nc.tensor

            def three(out, parts, full):
                n = 0
                for sh, sl, mh, ml in parts:
                    for s, m in ((sh, mh), (sh, ml), (sl, mh)):
                        ins = M.matmul(out, s, m, start=(n == 0), stop=(n == 3 * len(parts) - 1))
                        n += 1
                ins.then_inc(full, 1)

            def turn(n):
                pe.wait_ge(y_out, C * n + C)
                for i in range(2):
                    s = 2 * n + i
                    if s >= 2:
                        pe.wait_ge(t_out, s - 1)
                    for k in range(2):
                        for c in range(C):
                            last = M.transpose(bank[6 + i][:, D * k + P * c:D * k + P * c + P],
                                               g.x2[:, c, 2 * s + k, :], g.ident[:, :])
                    last.then_inc(t_full, 1)

            for n in range(NB):
                toks = slice(512 * n, 512 * n + 512)
                for m in range(M1):
                    if n == 0:
                        pe.wait_ge(wl_ready, 2 * (m // 4) + 2)
                    s = M1 * n + m
                    if s >= 4:
                        pe.wait_ge(gelu_ready, s - 3)
                    ms = slice(P * m, P * m + P)
                    three(bank[s % 4][:, :], [(w1_h[:, c, ms], w1_l[:, c, ms], xh[:, c, toks], xl[:, c, toks])
                                              for c in range(C)], f_full)
                if n:
                    turn(n - 1)
                pe.wait_ge(wl_ready, 8)
                pe.wait_ge(hl_ready, M1 * n + M1)
                for m in range(C):
                    s = C * n + m
                    if s >= 2:
                        pe.wait_ge(y_out, s - 1)
                    ms = slice(P * m, P * m + P)
                    three(bank[4 + m][:, :], [(w2_h[:, k, ms], w2_l[:, k, ms], h_h[:, k, :], h_l[:, k, :])
                                              for k in range(M1)], y_full)
            turn(NB - 1)

        @block.scalar
        def _(act):
            A = nc.scalar
            act.wait_ge(g.d_ff, 32)
            for i, (stage, hi, lo) in enumerate(pieces):
                A.activation(hi, stage, ACT.Copy).then_inc(wh_ready, 1)

            def gelu(s):
                act.wait_ge(f_full, s + 1)
                if s >= 2:
                    act.wait_ge(hl_ready, s - 1)
                A.activation(act_f[:, s % 2, :], bank[s % 4][:, :], ACT.Gelu,
                             bias=g.vec[:, V_B1 + s % M1:V_B1 + s % M1 + 1]).then_inc(gelu_ready, 1)

            def high(s):
                n, m = divmod(s, M1)
                act.wait_ge(gelu_ready, s + 1)
                if n:
                    act.wait_ge(y_full, C * n)
                A.activation(h_h[:, m, :], act_f[:, s % 2, :], ACT.Copy).then_inc(hh_ready, 1)

            for n in range(NB):
                gelu(M1 * n)
                for m in range(1, M1):
                    gelu(M1 * n + m)
                    high(M1 * n + m - 1)
                high(M1 * n + M1 - 1)

        @block.vector
        def _(dve):
            V = nc.vector
            for i, (stage, hi, lo) in enumerate(pieces):
                dve.wait_ge(wh_ready, i + 1)
                V.tensor_tensor(lo, stage, hi.bitcast(F32), SUB).then_inc(wl_ready, 1)

            def tokens_out(n):
                for i in range(2):
                    s = 2 * n + i
                    dve.wait_ge(t_full, s + 1)
                    if s >= 2:
                        dve.wait_ge(g.d_x3[i], 16 * (s // 2))
                    V.tensor_copy(x3_tok[:, i, :, :], bank[6 + i][:, :].rearrange("p (b f) -> p b f", b=2)).then_inc(t_out, 1)

            for n in range(NB):
                for m in range(M1):
                    s = M1 * n + m
                    dve.wait_ge(hh_ready, s + 1)
                    V.tensor_tensor(h_l[:, m, :], act_f[:, s % 2, :], h_h[:, m, :].bitcast(F32),
                                    SUB).then_inc(hl_ready, 1)
                if n:
                    tokens_out(n - 1)
                for m in range(C):
                    s = C * n + m
                    dve.wait_ge(y_full, s + 1)
                    dve.wait_ge(with_b, m + 1)
                    for i in range(BB):
                        b = BB * n + i
                        last = V.scalar_tensor_tensor(g.x2[:, m, b, :], bank[4 + m][:, T * i:T * i + T],
                                                      g.ada[:, 5 * C + m, b:b + 1], g.x2[:, m, b, :], MUL, ADD)
                    last.then_inc(y_out, 1)
            tokens_out(NB - 1)

        @block.gpsimd
        def _(pool):
            G = nc.gpsimd
            pool.wait_ge(g.d_keep, 32)
            for c in range(C):
                G.tensor_tensor(g.x2[:, c, :, :], g.x2[:, c, :, :], g.x2_in[:, c, :, :], ADD).then_inc(doubled, 1)
                G.tensor_scalar(gate_b[:, c, :], g.ada[:, 5 * C + c, :], g.vec[:, V_B2 + c:V_B2 + c + 1],
                                None, MUL).then_inc(gb_made, 1)
                pool.wait_ge(gb_made, c + 1)
                pool.wait_ge(doubled, c + 1)
                G.tensor_tensor(g.x2[:, c, :, :], g.x2[:, c, :, :],
                                gate_b[:, c, :].unsqueeze(2).broadcast_to([P, B, T]), ADD).then_inc(with_b, 1)

        @block.sync
        def _(sp):
            for s in range(2 * NB):
                sp.wait_ge(t_out, s + 1)
                sp.dma_start(x3_dram[2 * s:2 * s + 2, :, :].rearrange("b t f -> t b f"),
                             x3_tok[:, s % 2, :, :]).then_inc(g.d_x3[s % 2], 16)
            for i in range(2):
                sp.wait_ge(g.d_x3[i], 16 * NB)


def gru(nc, ctx, a, g, out, x3_dram):
    sb = lambda name, shape, dt=F32: ctx.enter_context(nc.sbuf_tensor(name, shape, dt))
    sem = lambda name: ctx.enter_context(nc.semaphore(name))
    J, E = 4, D // 4
    x3s = sb("x3s", [P, T, E])
    w_x = sb("w_x", [P, C, 3, D])
    w_h = sb("w_h", [P, C, 3, D])
    b_i, b_h = sb("b_i", [1, 3 * D]), sb("b_h", [1, 3 * D])
    bias = sb("bias3", [1, 4, D])
    ones = sb("ones3", [1, 32])
    h = [sb(f"h{i}", [P, E]) for i in range(2)]
    hT = sb("hT", [P, C, 32])
    xcol = sb("xcol", [P, 2, C, 32])
    rz = sb("rz", [P, 2 * E])
    rhn, pre, cand, keep, zh, new = (sb(n, [P, E]) for n in ("rhn", "pre", "cand", "keep", "zh", "new"))
    warm = sb("warm3", [P, 1])
    d_in, zeroed, bias_made, d_h0, d_x3s = sem("d_in3"), sem("zeroed3"), sem("bias_made3"), sem("d_h0"), sem("d_x3s")
    h_ready, hT_ready, g_full = sem("h_ready"), sem("hT_ready"), sem("g_full")
    xb_full = sem("xb_full")
    rz_ready, pre_ready, cand_ready = sem("rz_ready"), sem("pre_ready"), sem("cand_ready")
    x_ready, added = sem("xcol_ready"), sem("added")
    chain = sem("gru_chain")
    lap_done, lap_go, d_out = sem("lap_done3"), sem("lap_go3"), sem("d_out")
    NC = 4
    laps = T // LAP3
    bank = g.bank
    state = lambda d, j: d[:, :, E * j:E * j + E]

    def end_lap(eng, lap):
        eng.sem_inc(lap_done, 1)
        eng.wait_ge(lap_go, lap + 1)

    with nc.Block() as block:
        @block.sync
        def _(sp):
            for c in range(C):
                sp.dma_start(w_x[:, c, 0, :], a["L3_cond_W_ih"][P * c:P * c + P, 2 * D:]).then_inc(d_in, 16)
                sp.dma_start(w_x[:, c, 1:3, :].rearrange("p g n -> p (g n)"),
                             a["L3_cond_W_ih"][P * c:P * c + P, 0:2 * D]).then_inc(d_in, 16)
            for j in range(J):
                rows = a["L3_cond_W_hh"][E * j:E * j + E, :].rearrange("(c f) n -> f c n", f=32)
                sp.dma_start(w_h[32 * j:32 * j + 32, :, :, :].rearrange("p c g n -> p c (g n)"), rows).then_inc(d_in, 16)
            sp.dma_start(b_i[:, :], a["L3_cond_b_ih"].rearrange("(o n) -> o n", o=1)).then_inc(d_in, 16)
            sp.dma_start(b_h[:, :], a["L3_cond_b_hh"].rearrange("(o n) -> o n", o=1)).then_inc(d_in, 16)
            sp.wait_ge(zeroed, 4)
            for j in range(J):
                sp.dma_start(h[0][32 * j:32 * j + B, :], a["cond_2048"][:, E * j:E * j + E]).then_inc(d_h0, 16)
            for j in range(J):
                sp.dma_start(x3s[32 * j:32 * j + B, :, :], state(x3_dram, j)).then_inc(d_x3s, 16)
            with sp.Fori(0, laps) as lap:
                sp.wait_ge(lap_done, lap * 4 + 4)
                for s, n in ((h_ready, 1), (hT_ready, 1), (g_full, 1), (xb_full, 1), (rz_ready, 1),
                             (pre_ready, 1), (cand_ready, 1), (x_ready, 1), (added, 1), (chain, NC)):
                    sp.sem_inc(s, -n * LAP3)
                sp.sem_inc(lap_go, 1)
                for j in range(J):
                    o = state(out, j)[:, bass.ds(lap * LAP3, LAP3), :]
                    sp.dma_start(o, x3s[32 * j:32 * j + B, bass.ds(lap * LAP3, LAP3), :]).then_inc(d_out, 16)
            sp.wait_ge(d_out, 16 * J * laps)

        @block.gpsimd
        def _(pool):
            G = nc.gpsimd
            for i in range(2):
                G.memset(h[i][:, :], 0.0).then_inc(zeroed, 1)
            G.memset(xcol[:, :, :, :], 0.0).then_inc(zeroed, 1)
            G.memset(x3s[:, :, :], 0.0).then_inc(zeroed, 1)
            pool.wait_ge(d_x3s, 16 * J)
            pool.wait_ge(zeroed, 4)
            x3 = g.x2[:, :, :, :]

            with pool.Fori(0, laps) as lap:
                def column(j):
                    if j >= 2:
                        pool.wait_ge(xb_full, j - 1)
                    G.tensor_copy(xcol[:, j % 2, :, 0:B].unsqueeze(3),
                                  x3[:, :, :, bass.ds(lap * LAP3 + j, 1)]).then_inc(x_ready, 1)

                column(0)
                for j in range(LAP3):
                    if j + 1 < LAP3:
                        column(j + 1)
                    pool.wait_ge(h_ready, j + 2)
                    t = x3s[:, bass.ds(lap * LAP3 + j, 1), :].rearrange("p t e -> p (t e)")
                    G.tensor_tensor(t, t, h[(j + 1) % 2][:, :], ADD).then_inc(added, 1)
                pool.wait_ge(added, LAP3)
                end_lap(pool, lap)

        @block.tensor
        def _(pe):
            M = nc.tensor
            pe.wait_ge(d_in, 16 * (2 * C + J + 2))
            pe.wait_ge(bias_made, 5)
            with pe.Fori(0, laps) as lap:
                def inputs(s):
                    if s >= 2:
                        pe.wait_ge(pre_ready, s - 1)
                        pe.wait_ge(rz_ready, s - 1)
                    gates = lambda j, lo, n: bank[s % 2][32 * j:32 * j + 32, E * lo:E * lo + E * n].rearrange(
                        "p (g e) -> p g e", e=E)
                    for j in range(J):
                        M.matmul(gates(j, 0, 4), ones[:, :], bias[:, :, E * j:E * j + E], start=True, stop=False,
                                 skip_group_check=True)
                    pe.wait_ge(x_ready, s + 1)
                    for j in range(J):
                        for c in range(C):
                            last = M.matmul(gates(j, 0, 3), xcol[:, s % 2, c, :], w_x[:, c, :, E * j:E * j + E],
                                            start=False, stop=False, skip_group_check=True)
                    last.then_inc(xb_full, 1)

                inputs(0)
                for s in range(LAP3):
                    pe.wait_ge(hT_ready, s + 1)
                    for j in range(J):
                        for c in range(C):
                            o = bank[s % 2][32 * j:32 * j + 32, E:4 * E].rearrange("p (g e) -> p g e", e=E)
                            last = M.matmul(o, hT[:, c, :], w_h[:, c, :, E * j:E * j + E], start=False,
                                            stop=(c == C - 1), skip_group_check=True)
                    last.then_inc(g_full, 1)
                    if s + 1 < LAP3:
                        inputs(s + 1)
                end_lap(pe, lap)

        @block.scalar
        def _(act):
            A = nc.scalar
            A.activation(warm[:, :], g.eps6[:, :], ACT.Sigmoid)
            with act.Fori(0, laps) as lap:
                for s in range(LAP3):
                    act.wait_ge(g_full, s + 1)
                    A.activation(rz[:, :], bank[s % 2][:, E:3 * E], ACT.Sigmoid).then_inc(rz_ready, 1)
                    act.wait_ge(pre_ready, s + 1)
                    A.activation(cand[:, :], pre[:, :], ACT.Tanh).then_inc(cand_ready, 1)
                end_lap(act, lap)

        @block.vector
        def _(dve):
            V = nc.vector
            V.memset(ones[:, :], 1.0).then_inc(bias_made, 1)
            dve.wait_ge(d_in, 16 * (2 * C + J + 2))
            V.tensor_copy(bias[:, 0, :], b_i[:, 2 * D:]).then_inc(bias_made, 1)
            V.tensor_copy(bias[:, 3, :], b_h[:, 2 * D:]).then_inc(bias_made, 1)
            for gate in range(2):
                gs = slice(D * gate, D * gate + D)
                V.tensor_tensor(bias[:, 1 + gate, :], b_i[:, gs], b_h[:, gs], ADD).then_inc(bias_made, 1)
            dve.wait_ge(d_h0, 16 * J)
            dve.sem_inc(h_ready, 1)
            with dve.Fori(0, laps) as lap:
                for s in range(LAP3):
                    def do(ins, n):
                        ins.then_inc(chain, 1)

                    n0 = NC * s
                    dve.wait_ge(h_ready, s + 1)
                    V.transpose(hT[:, :, :].rearrange("p c b -> p (c b)"), h[s % 2][:, :]).then_inc(hT_ready, 1)
                    dve.wait_ge(rz_ready, s + 1)
                    V.tensor_tensor(rhn[:, :], rz[:, 0:E], bank[s % 2][:, 3 * E:4 * E], MUL).then_inc(chain, 1)
                    dve.wait_ge(chain, n0 + 1)
                    V.tensor_tensor(pre[:, :], rhn[:, :], bank[s % 2][:, 0:E], ADD).then_inc(pre_ready, 1)
                    V.tensor_scalar(keep[:, :], rz[:, E:2 * E], -1.0, 1.0, MUL, ADD).then_inc(chain, 1)
                    V.tensor_tensor(zh[:, :], rz[:, E:2 * E], h[s % 2][:, :], MUL).then_inc(chain, 1)
                    dve.wait_ge(cand_ready, s + 1)
                    dve.wait_ge(chain, n0 + 3)
                    V.tensor_tensor(new[:, :], cand[:, :], keep[:, :], MUL).then_inc(chain, 1)
                    dve.wait_ge(chain, n0 + 4)
                    if s >= 2:
                        dve.wait_ge(added, s - 1)
                    V.tensor_tensor(h[(s + 1) % 2][:, :], new[:, :], zh[:, :], ADD).then_inc(h_ready, 1)
                dve.wait_ge(h_ready, LAP3 + 1)
                end_lap(dve, lap)


class Shared:
    pass


def layers(nc, a, out):
    g = Shared()
    with ExitStack() as whole:
        def sb(ctx, name, shape, dt=F32):
            return ctx.enter_context(nc.sbuf_tensor(name, shape, dt))

        sem = lambda name: whole.enter_context(nc.semaphore(name))
        g.bank = [whole.enter_context(nc.psum_tensor(f"bank{i}", [P, 512], F32)) for i in range(8)]
        g.ident = sb(whole, "ident", [P, P])
        g.mean_w = sb(whole, "mean_w", [P, P])
        g.block_w = sb(whole, "block_w", [P, P])
        g.eps6 = sb(whole, "eps6", [P, 1])
        g.condT = sb(whole, "condT", [P, C, B])
        g.vec = sb(whole, "vec", [P, V_ROWS])
        g.coup_scale = sb(whole, "coup_scale", [P, 4])
        g.coup_hi = sb(whole, "coup_hi", [P, C * D], F16)
        g.coup_lo = sb(whole, "coup_lo", [P, C * D], F16)
        g.gain0 = sb(whole, "gain0", [P, C, B])
        g.shift0 = sb(whole, "shift0", [P, C, B])
        g.ada = sb(whole, "ada", [P, 6 * C, B])
        g.drive_b = sb(whole, "drive_b", [P, C])
        g.x2 = sb(whole, "x2", [P, C, B, T])
        g.d_w0, g.d_ada = sem("d_w0"), sem("d_ada")
        g.d_w2, g.d_ow, g.d_ff = sem("d_w2"), sem("d_ow"), sem("d_ff")
        g.d_x3 = [sem(f"d_x3tok{i}") for i in range(2)]
        g.d_keep = sem("d_keep")
        g.d_vb = [sem(f"d_vb{i}") for i in range(4)]
        x3_dram = nc.dram_tensor("x3_tokens", [B, T, D], F32, kind="Internal").ap()
        x2_dram = nc.dram_tensor("x2_in", [P, C, B, T], F32, kind="Internal").ap()
        with ExitStack() as scan:
            g.x1 = sb(scan, "x1", [P, T, C, B])
            g.drive = sb(scan, "drive", [P, T, C, B])
            with ExitStack() as layer0:
                g.w_out0 = sb(layer0, "w_out0", [P, C, D])
                g.w_qkv0 = sb(layer0, "w_qkv0", [P, C, 3 * D])
                g.ada_w = sb(layer0, "ada_w", [P, C, 6 * D])
                g.xT = sb(layer0, "xT", [P, C, B, T])
                g.xm = sb(layer0, "xm", [P, C, B, T])
                with ExitStack() as ctx:
                    prepare(nc, ctx, a, g)
                g.q0 = sb(layer0, "q0", [P, C, TOK])
                g.k0 = [sb(layer0, f"k0_{i}", [P, C, TOK]) for i in range(2)]
                g.v0 = sb(layer0, "v0", [P, 2, B, D])
                with ExitStack() as ctx:
                    project0(nc, ctx, a, g)
                with ExitStack() as ctx:
                    attend0(nc, ctx, a, g)
            g.trace = sb(scan, "trace", [P, T + 1, C, B])
            with ExitStack() as ctx:
                scan1(nc, ctx, a, g)
        with ExitStack() as layer2:
            xh = sb(layer2, "x_hi", [P, C, TOK], F32R)
            xl = sb(layer2, "x_lo", [P, C, TOK], F32R)
            with ExitStack() as heads:
                g.w_stage = sb(heads, "w2_stage", [P, 3, C, 512])
                g.ow_stage = sb(heads, "ow_stage", [P, 4, D])
                g.v_bias = sb(heads, "v_bias", [P, 2, 512])

                def loads(sp):
                    load_w2(sp, a, g, 0)
                    load_ow(sp, a, g, 0)
                    load_vb(sp, a, g, 0)
                    sp.dma_start(x2_dram, g.x2[:, :, :, :]).then_inc(g.d_keep, 16)
                    sp.wait_ge(g.d_keep, 16)

                with ExitStack() as ctx:
                    norm_split(nc, ctx, a, g, "_a", 1, 0, xh, xl, loads)
                with ExitStack() as ctx:
                    attend2(nc, ctx, a, g, xh, xl)
            g.w1_stage = sb(layer2, "w1_stage", [P, C, FF])
            g.x2_in = sb(layer2, "x2_in_sb", [P, C, B, T])
            g.ffw2_stage = sb(layer2, "ffw2_stage", [P, FF // P, D])

            def loads(sp):
                sp.dma_start(g.w1_stage[:, :, :],
                             a["L2_cond_ffn_w1"].rearrange("(c p) n -> p c n", p=P)).then_inc(g.d_ff, 16)
                sp.dma_start(g.ffw2_stage[:, :, :],
                             a["L2_cond_ffn_w2"].rearrange("(k p) n -> p k n", p=P)).then_inc(g.d_ff, 16)
                sp.dma_start(g.x2_in[:, :, :, :], x2_dram).then_inc(g.d_keep, 16)

            with ExitStack() as ctx:
                norm_split(nc, ctx, a, g, "_b", 4, 3, xh, xl, loads)
            with ExitStack() as ctx:
                feed_forward(nc, ctx, a, g, xh, xl, x3_dram)
        with ExitStack() as ctx:
            gru(nc, ctx, a, g, out, x3_dram)


_INS = ["x", "cond_2048", "L0_cond_W_emb", "L0_cond_b_emb", "L0_cond_g_norm", "L0_cond_W_qkv", "L0_cond_g_q",
        "L0_cond_g_k", "L0_cond_W_out", "L1_cond_coupling", "L1_cond_bias", "L2_cond_ada_w", "L2_cond_ada_b",
        "L2_cond_qkv_w", "L2_cond_qkv_b", "L2_cond_out_w", "L2_cond_out_b", "L2_cond_ffn_w1", "L2_cond_ffn_b1",
        "L2_cond_ffn_w2", "L2_cond_ffn_b2", "L3_cond_W_ih", "L3_cond_W_hh", "L3_cond_b_ih", "L3_cond_b_hh"]


def kernel(**inputs):
    import numpy as _np
    import concourse.bacc as _bacc
    from concourse import mybir as _mybir
    from concourse.bass_utils import run_bass_kernel_spmd as _run

    nc = _bacc.Bacc("TRN2", target_bir_lowering=False, num_devices=1)
    arrays, aps = {}, {}
    for name in _INS:
        a = _np.ascontiguousarray(inputs[name])
        arrays[f"in_{name}_dram"] = a
        aps[name] = nc.dram_tensor(f"in_{name}_dram", a.shape, _mybir.dt.from_np(a.dtype), kind="ExternalInput").ap()
    out = nc.dram_tensor("out_0_dram", (B, T, D), F32, kind="ExternalOutput").ap()
    layers(nc, aps, out)
    r = _run(nc, [arrays], core_ids=[0])
    return r.results[0]["out_0_dram"]
```

```python
from contextlib import ExitStack

import concourse.bass as bass
from concourse import mybir

F32 = mybir.dt.float32
F32R = mybir.dt.float32r
F16 = mybir.dt.float16
ACT = mybir.ActivationFunctionType
ALU = mybir.AluOpType
AX_X = mybir.AxisListType.X
MUL, ADD, SUB = ALU.mult, ALU.add, ALU.subtract

P = 128
B, T, D = 16, 128, 256
C = D // P
TOK = B * T
NB = TOK // 512
BB = B // NB
H0, D0 = 16, 16
H2, D2 = 16, 128
FF = 4 * D
DT, EPSILON, ALPHA, BETA, CLAMP = 0.01, 0.08, 0.7, 0.8, 20.0
EPS = 1e-6
W1 = C * B
LAP = 32
LAP3 = 32

V_GNORM, V_BEMB, V_BIAS1, V_ADAB, V_QKB, V_OUTB, V_B1, V_B2, V_GQ, V_GK, V_ROWS = (
    0, 2, 6, 8, 20, 52, 54, 62, 64, 65, 66)


class Count:

    def __init__(self, eng, sem):
        self.eng, self.sem, self.n = eng, sem, 0

    def __call__(self, ins):
        ins.then_inc(self.sem, 1)
        self.n += 1
        return self.n

    def wait(self, n):
        self.eng.wait_ge(self.sem, n)


def prepare(nc, ctx, a, g):
    sb = lambda name, shape, dt=F32: ctx.enter_context(nc.sbuf_tensor(name, shape, dt))
    sem = lambda name: ctx.enter_context(nc.semaphore(name))
    cond = sb("cond", [B, D])
    rows = sb("rows", [V_ROWS, P])
    x_tok = sb("x_tok", [P, B, D])
    xn_tok = sb("xn_tok", [P, B, D])
    square = sb("square", [P, 2, D])
    sum_sq = sb("sum_sq", [P, B])
    log_ms = sb("log_ms", [P, B])
    rstd = sb("rstd", [P, B])
    w_emb = sb("w_emb", [P, C, 2 * D])
    coup = sb("coup", [P, C, D])
    coup_abs = sb("coup_abs", [P, 1])
    coup_row = sb("coup_row", [1, P])
    coup_top = sb("coup_top", [1, 1])
    ones_row = sb("ones_row", [1, P])
    coup_inv = sb("coup_inv", [P, 1])
    coup_n = sb("coup_n", [P, C * D])
    gain = sb("gain", [P, C, B])
    d_x = [sem(f"d_x{n}") for n in range(NB)]
    d_cond, d_rows, d_emb, d_coup = sem("d_cond"), sem("d_rows"), sem("d_emb"), sem("d_coup")
    consts_made = sem("consts_made")
    pool_made = sem("pool_made")
    sq_done = sem("sq_done")
    act_chain = sem("act_chain")
    dve_chain = sem("dve_chain")
    rstd_ready = sem("rstd_ready")
    xn_ready = sem("xn_ready")
    small_full = sem("small_full")
    small_out = sem("small_out")
    xn_full, xn_out = sem("xn_full"), sem("xn_out")
    x_full, x_out = sem("x_full"), sem("x_out")
    x_in = a["x"].rearrange("b t f -> t b f")
    bank = g.bank

    with nc.Block() as block:
        @block.sync
        def _(sp):
            sp.dma_start(cond[:, :], a["cond_2048"]).then_inc(d_cond, 16)
            for n in range(NB):
                bs = slice(BB * n, BB * n + BB)
                sp.dma_start(x_tok[:, bs, :], x_in[:, bs, :]).then_inc(d_x[n], 16)
            by_chunk = lambda w: w.rearrange("(c p) n -> p c n", p=P)
            sp.dma_start(w_emb[:, :, :], by_chunk(a["L0_cond_W_emb"])).then_inc(d_emb, 16)
            sp.dma_start(coup[:, :, :], by_chunk(a["L1_cond_coupling"])).then_inc(d_coup, 16)
            sp.dma_start(g.w_qkv0[:, :, :], by_chunk(a["L0_cond_W_qkv"])).then_inc(g.d_w0, 16)
            sp.dma_start(g.w_out0[:, :, :], by_chunk(a["L0_cond_W_out"])).then_inc(g.d_w0, 16)
            sp.dma_start(g.ada_w[:, :, :], by_chunk(a["L2_cond_ada_w"])).then_inc(g.d_ada, 16)

        @block.gpsimd
        def _(pool):
            made = Count(pool, pool_made)
            G = nc.gpsimd
            made(G.memset(g.ident[:, :], 0.0))
            made(G.memset(g.mean_w[:, :], 1.0 / D))
            n = made(G.memset(g.block_w[:, :], 1.0 / D0))
            made.wait(n)
            made(G.affine_select(out=g.ident[:, :], in_=g.ident[:, :], compare_op=ALU.not_equal,
                                 fill=1.0, base=0, pattern=[[-1, P]], channel_multiplier=1))
            blocks = g.block_w[:, :].rearrange("p (h e) -> p h e", e=D0)
            n = made(G.affine_select(out=blocks, in_=blocks, compare_op=ALU.is_ge, fill=0.0, base=0,
                                     pattern=[[-D0, P // D0], [0, D0]], channel_multiplier=1))
            made.wait(n)
            n = made(G.affine_select(out=blocks, in_=blocks, compare_op=ALU.is_ge, fill=0.0,
                                     base=D0 - 1, pattern=[[D0, P // D0], [0, D0]],
                                     channel_multiplier=-1))
            made.wait(n)
            G.memset(ones_row[:, :], 1.0).then_inc(consts_made, 1)

        @block.scalar
        def _(act):
            A = nc.scalar
            row = lambda v, n: rows[v:v + n, :]
            stack = lambda w: w.rearrange("(r p) -> r p", p=P)
            for v, w in ((V_GNORM, "L0_cond_g_norm"), (V_BEMB, "L0_cond_b_emb"),
                         (V_BIAS1, "L1_cond_bias"), (V_ADAB, "L2_cond_ada_b"),
                         (V_OUTB, "L2_cond_out_b"), (V_B1, "L2_cond_ffn_b1"),
                         (V_B2, "L2_cond_ffn_b2")):
                act.dma_start(row(v, a[w].shape[0] // P), stack(a[w])).then_inc(d_rows, 16)
            act.dma_start(row(V_QKB, 2 * H2), stack(a["L2_cond_qkv_b"][0:2 * H2 * D2])).then_inc(d_rows, 16)
            for v, w in ((V_GQ, "L0_cond_g_q"), (V_GK, "L0_cond_g_k")):
                tiled = a[w].rearrange("(o e) -> o e", o=1).unsqueeze(1).broadcast_to([1, P // D0, D0])
                act.dma_start(row(v, 1).rearrange("o (h e) -> o h e", e=D0), tiled).then_inc(d_rows, 16)
            chain = Count(act, act_chain)
            for b in range(B):
                act.wait_ge(d_x[b // BB], 16)
                if b >= 2:
                    chain.wait(b - 1)
                n = chain(A.activation(square[:, b % 2, :], x_tok[:, b, :], ACT.Square,
                                       accum_out=sum_sq[:, b:b + 1]))
            chain.wait(n)
            act.wait_ge(dve_chain, 1)
            n = chain(A.activation(log_ms[:, :], sum_sq[:, :], ACT.Ln, bias=g.eps6[:, :], scale=1.0 / D))
            chain.wait(n)
            A.activation(rstd[:, :], log_ms[:, :], ACT.Exp, scale=-0.5).then_inc(rstd_ready, 1)
            for n in range(2 * NB):
                act.wait_ge(x_full, n + 1)
                A.activation(g.xT[:, n // NB, BB * (n % NB):BB * (n % NB) + BB, :],
                             bank[4 + n % 2][:, :], ACT.Copy).then_inc(x_out, 1)

        @block.vector
        def _(dve):
            V = nc.vector
            chain = Count(dve, dve_chain)
            chain(V.memset(g.eps6[:, :], EPS))
            dve.wait_ge(small_full, 1)
            V.tensor_copy(g.condT[:, :, :], bank[0][:, 0:W1]).then_inc(small_out, 1)
            dve.wait_ge(small_full, 2)
            V.tensor_copy(g.vec[:, :], bank[1][:, 0:V_ROWS]).then_inc(small_out, 1)
            dve.wait_ge(d_coup, 16)
            V.tensor_reduce(coup_abs[:, :], coup[:, :, :].rearrange("p c n -> p (c n)"), op=ALU.max,
                            axis=AX_X, apply_absolute_value=True).then_inc(small_out, 1)
            dve.wait_ge(small_full, 4)
            V.tensor_reduce(coup_top[:, :], bank[3][0:1, 0:P], op=ALU.max, axis=AX_X).then_inc(small_out, 1)
            dve.wait_ge(small_full, 5)
            n = chain(V.tensor_scalar(g.coup_scale[:, 3:4], bank[0][:, 0:1], 1e-30, None, ALU.max))
            chain.wait(n)
            for i, step in enumerate((DT / 2, DT, DT / 6)):
                chain(V.tensor_scalar(g.coup_scale[:, i:i + 1], g.coup_scale[:, 3:4], step, None, MUL))
            n = chain(V.reciprocal(coup_inv[:, :], g.coup_scale[:, 3:4]))
            chain.wait(n)
            n = chain(V.tensor_scalar(coup_n[:, :], bank[2][:, :], coup_inv[:, 0:1], None, MUL))
            chain.wait(n)
            n = chain(V.tensor_copy(g.coup_hi[:, :], coup_n[:, :]))
            chain.wait(n)
            chain(V.tensor_tensor(g.coup_lo[:, :], coup_n[:, :], g.coup_hi[:, :], SUB))
            dve.wait_ge(small_full, 6)
            for m in range(2 * C):
                src = bank[1][:, B * m:B * m + B]
                bias = g.vec[:, V_BEMB + m:V_BEMB + m + 1]
                if m < C:
                    n = chain(V.tensor_scalar(gain[:, m, :], src, bias, 1.0, ADD, ADD))
                else:
                    chain(V.tensor_scalar(g.shift0[:, m - C, :], src, bias, None, ADD))
            chain.wait(n)
            for c in range(C):
                n = chain(V.tensor_scalar(g.gain0[:, c, :], gain[:, c, :],
                                          g.vec[:, V_GNORM + c:V_GNORM + c + 1], None, MUL))
            dve.wait_ge(rstd_ready, 1)
            for b in range(B):
                V.tensor_scalar(xn_tok[:, b, :], x_tok[:, b, :], rstd[:, b:b + 1], None,
                                MUL).then_inc(xn_ready, 1)
            chain.wait(n)
            for n in range(2 * NB):
                dve.wait_ge(xn_full, n + 1)
                c = n // NB
                for i in range(BB):
                    b = BB * (n % NB) + i
                    last = V.tensor_scalar(g.xm[:, c, b, :], bank[6 + n % 2][:, P * i:P * i + P],
                                           g.gain0[:, c, b:b + 1], g.shift0[:, c, b:b + 1], MUL, ADD)
                last.then_inc(xn_out, 1)

        @block.tensor
        def _(pe):
            M = nc.tensor
            pe.wait_ge(pool_made, 4)
            pe.wait_ge(d_cond, 16)
            for c in range(C):
                last = M.transpose(bank[0][:, B * c:B * c + B], cond[:, P * c:P * c + P], g.ident[0:B, 0:B])
            last.then_inc(small_full, 1)
            pe.wait_ge(d_rows, 16 * 10)
            M.transpose(bank[1][:, 0:V_ROWS], rows[:, :], g.ident[0:V_ROWS, 0:V_ROWS]).then_inc(small_full, 1)
            pe.wait_ge(d_coup, 16)
            for cm in range(C):
                for cn in range(C):
                    o = D * cm + P * cn
                    last = M.transpose(bank[2][:, o:o + P], coup[:, cn, P * cm:P * cm + P], g.ident[:, :])
            last.then_inc(small_full, 1)
            pe.wait_ge(small_out, 3)
            M.transpose(bank[3][0:1, 0:P], coup_abs[:, :], g.ident[:, :]).then_inc(small_full, 1)
            pe.wait_ge(small_out, 4)
            pe.wait_ge(consts_made, 1)
            M.matmul(bank[0][:, 0:1], ones_row[:, :], coup_top[:, :], start=True, stop=True).then_inc(small_full, 1)
            pe.wait_ge(d_emb, 16)
            for m in range(2 * C):
                for c in range(C):
                    last = M.matmul(bank[1][:, B * m:B * m + B], w_emb[:, c, P * m:P * m + P],
                                    g.condT[:, c, :], start=(c == 0), stop=(c == C - 1))
            last.then_inc(small_full, 1)

            def tiles(src, n, out, full):
                c = n // NB
                for i in range(BB):
                    last = M.transpose(out[:, P * i:P * i + P], src[:, BB * (n % NB) + i, P * c:P * c + P],
                                       g.ident[:, :])
                last.then_inc(full, 1)

            for n in range(2 * NB):
                pe.wait_ge(d_x[n % NB], 16)
                if n >= 2:
                    pe.wait_ge(x_out, n - 1)
                tiles(x_tok, n, bank[4 + n % 2], x_full)
            for n in range(2 * NB):
                pe.wait_ge(xn_ready, BB * (n % NB) + BB)
                if n >= 2:
                    pe.wait_ge(xn_out, n - 1)
                tiles(xn_tok, n, bank[6 + n % 2], xn_full)


def project0(nc, ctx, a, g):
    sb = lambda name, shape, dt=F32: ctx.enter_context(nc.sbuf_tensor(name, shape, dt))
    sem = lambda name: ctx.enter_context(nc.semaphore(name))
    square = sb("square0", [P, 2, 512])
    rstd = [g.x1[:, :, :, :].rearrange("p t c b -> p (t c b)"), g.x2_flat[:, 0:C * TOK]]
    even = sb("even", [P, 1])
    odd = sb("odd", [P, 1])
    gains = sb("gains", [P, 3])
    raw_full, raw_out = sem("raw_full"), sem("raw_out")
    sq_ready, ms_full, log_ready, rstd_ready = sem("sq_ready"), sem("ms_full"), sem("log_ready0"), sem("rstd_ready0")
    dve_chain, odd_made = sem("dve_chain0"), sem("odd_made")
    v_full, v_out = sem("v_full"), sem("v_out")
    zeroed = sem("zeroed")
    units = [(w, m, n) for w in range(2) for m in range(C) for n in range(NB)]
    bank = g.bank

    def place(t, u):
        w, m, n = units[u]
        return t[:, m, 512 * n:512 * n + 512]

    xm = lambda c, n: g.xm[:, c, BB * n:BB * n + BB, :].rearrange("p b t -> p (b t)")

    with nc.Block() as block:
        @block.gpsimd
        def _(pool):
            nc.gpsimd.memset(g.v0[:, :, :, :], 0.0).then_inc(zeroed, 1)

        @block.tensor
        def _(pe):
            M = nc.tensor
            pe.wait_ge(g.d_w0, 32)

            def mean_square(u):
                pe.wait_ge(sq_ready, u + 1)
                if u >= 2:
                    pe.wait_ge(log_ready, u - 1)
                M.matmul(bank[4 + u % 2][:, :], g.block_w[:, :], square[:, u % 2, :], start=True,
                         stop=True).then_inc(ms_full, 1)

            for u, (w, m, n) in enumerate(units):
                if u >= 4:
                    pe.wait_ge(raw_out, u - 3)
                for c in range(C):
                    o = D * w + P * m
                    last = M.matmul(bank[u % 4][:, :], g.w_qkv0[:, c, o:o + P], xm(c, n),
                                    start=(c == 0), stop=(c == C - 1))
                last.then_inc(raw_full, 1)
                if u:
                    mean_square(u - 1)
            mean_square(len(units) - 1)
            for i in range(B // 2):
                if i >= 2:
                    pe.wait_ge(v_out, i - 1)
                for k in range(2):
                    for c in range(C):
                        last = M.matmul(bank[6 + i % 2][:, D * k:D * k + D], g.xm[:, c, 2 * i + k, :],
                                        g.w_qkv0[:, c, 2 * D:3 * D], start=(c == 0), stop=(c == C - 1))
                last.then_inc(v_full, 1)

        @block.scalar
        def _(act):
            A = nc.scalar
            def logarithm(u):
                act.wait_ge(ms_full, u + 1)
                A.activation(rstd[u // 8][:, 512 * (u % 8):512 * (u % 8) + 512], bank[4 + u % 2][:, :], ACT.Ln,
                             bias=g.eps6[:, :]).then_inc(log_ready, 1)

            for w in range(2):
                for u in range(8 * w, 8 * w + 8):
                    act.wait_ge(raw_out, u + 1)
                    if u >= 2:
                        act.wait_ge(ms_full, u - 1)
                    A.activation(square[:, u % 2, :], place(g.q0 if w == 0 else g.k0[0], u), ACT.Square).then_inc(sq_ready, 1)
                    if u > 8 * w:
                        logarithm(u - 1)
                logarithm(8 * w + 7)
                act.wait_ge(log_ready, 8 * w + 8)
                for i in range(2):
                    part = rstd[w][:, 2048 * i:2048 * i + 2048]
                    A.activation(part, part, ACT.Exp, scale=-0.5).then_inc(rstd_ready, 1)
            act.wait_ge(zeroed, 1)
            for i in range(B // 2):
                act.wait_ge(v_full, i + 1)
                src = bank[6 + i % 2][:, :].rearrange("p (b h e) -> p b h e", b=2, e=D0)
                for odd_heads in range(2):
                    dst = g.v0[:, odd_heads, 2 * i:2 * i + 2, :].rearrange("p b (h e) -> p b h e", e=D0)
                    last = A.activation(dst[:, :, odd_heads::2, :], src[:, :, odd_heads::2, :], ACT.Copy)
                last.then_inc(v_out, 1)

        @block.vector
        def _(dve):
            V = nc.vector
            chain = Count(dve, dve_chain)
            heads = g.block_w[:, :].rearrange("p (h e) -> p h e", e=D0)
            n = chain(V.tensor_reduce(even[:, :], heads[:, ::2, 0], op=ADD, axis=AX_X))
            chain.wait(n)
            n = chain(V.tensor_scalar(even[:, :], even[:, :], float(D0), None, MUL))
            chain.wait(n)
            n = chain(V.tensor_scalar(odd[:, :], even[:, :], -1.0, 1.0, MUL, ADD))
            chain.wait(n)
            chain(V.tensor_scalar(gains[:, 0:1], g.vec[:, V_GQ:V_GQ + 1], D0 ** -0.5, None, MUL))
            chain(V.tensor_tensor(gains[:, 1:2], g.vec[:, V_GK:V_GK + 1], even[:, :], MUL))
            n = chain(V.tensor_tensor(gains[:, 2:3], g.vec[:, V_GK:V_GK + 1], odd[:, :], MUL))
            chain.wait(n)
            def normalise(dst, src, gain, u):
                dve.wait_ge(rstd_ready, u // 4 + 1)
                return V.scalar_tensor_tensor(place(dst, u), place(src, u), gains[:, gain:gain + 1],
                                              rstd[u // 8][:, 512 * (u % 8):512 * (u % 8) + 512], MUL, MUL)

            for u in range(16):
                dve.wait_ge(raw_full, u + 1)
                V.tensor_copy(place(g.q0 if u < 8 else g.k0[0], u), bank[u % 4][:, :]).then_inc(raw_out, 1)
                if u >= 12:
                    for v in range(2 * (u - 12), 2 * (u - 12) + 2):
                        normalise(g.q0, g.q0, 0, v)
            dve.wait_ge(raw_out, 16)
            for u in range(8, 16):
                normalise(g.k0[1], g.k0[0], 2, u).then_inc(odd_made, 1)
            for u in range(8, 16):
                dve.wait_ge(odd_made, u - 7)
                normalise(g.k0[0], g.k0[0], 1, u)


def attend0(nc, ctx, a, g):
    sb = lambda name, shape, dt=F32: ctx.enter_context(nc.sbuf_tensor(name, shape, dt))
    sem = lambda name: ctx.enter_context(nc.semaphore(name))
    neg_max = sb("neg_max0", [P, 4, 4])
    sums = sb("sums0", [P, 4, 4])
    inv = sb("inv0", [P, 4, 4])
    prob = sb("prob0", [P, 6, 4, T])
    probT = sb("probT0", [P, 4, 512])
    o0 = g.xm
    w_res = sb("w_res0", [P, C, D])
    s_full, max_ready, p_ready = sem("s_full"), sem("max_ready"), sem("p_ready")
    inv_ready, pn_ready = sem("inv_ready"), sem("pn_ready")
    t_full, t_out, o_full, o_out = sem("t_full"), sem("t_out"), sem("o_full"), sem("o_out")
    w_made, y_full, y_out = sem("w_made"), sem("y_full"), sem("y_out")
    ada_full, ada_out = sem("ada_full"), sem("ada_out")
    bias_made, w_copied = sem("bias_made"), sem("w_copied")
    bank = g.bank
    U = B * 4

    with nc.Block() as block:
        @block.tensor
        def _(pe):
            M = nc.tensor
            pe.wait_ge(g.d_ada, 16)
            for m in range(6 * C):
                for c in range(C):
                    last = M.matmul(bank[7][:, B * m:B * m + B], g.ada_w[:, c, P * m:P * m + P],
                                    g.condT[:, c, :], start=(c == 0), stop=(c == C - 1))
            last.then_inc(ada_full, 1)

            def scores(w):
                if w >= 2:
                    pe.wait_ge(p_ready, 2 * w - 2)
                for i in range(4):
                    for u in (2 * w, 2 * w + 1):
                        b, r = divmod(u, 4)
                        rs = slice(32 * r, 32 * r + 32)
                        last = M.matmul(bank[u % 4][:, T * i:T * i + T], g.q0[rs, i // 2, T * b:T * b + T],
                                        g.k0[i % 2][rs, i // 2, T * b:T * b + T], start=True, stop=True)
                last.then_inc(s_full, 1)

            def turn(u):
                pe.wait_ge(pn_ready, u + 1)
                if u >= 2:
                    pe.wait_ge(t_out, u - 1)
                for i in range(4):
                    last = M.transpose(bank[4 + u % 2][:, T * i:T * i + T], prob[:, u % 6, i, :], g.ident[:, :])
                last.then_inc(t_full, 1)

            def weigh(w):
                b = w // 2
                pe.wait_ge(t_out, 2 * w + 2)
                if b == 1:
                    pe.wait_ge(ada_out, 1)
                if w % 2 == 0 and b >= 2:
                    pe.wait_ge(o_out, b - 1)
                for i in range(4):
                    m, e = divmod(i, 2)
                    for u in (2 * w, 2 * w + 1):
                        r = u % 4
                        last = M.matmul(bank[6 + b % 2][32 * r:32 * r + 32, T * m:T * m + T],
                                        g.v0[:, e, b, P * m + 32 * r:P * m + 32 * r + 32],
                                        probT[:, u % 4, T * i:T * i + T], start=(e == 0), stop=(e == 1))
                last.then_inc(o_full, 1)

            for w in range(U // 2 + 3):
                if w < U // 2:
                    scores(w)
                if 2 <= w < U // 2 + 2:
                    turn(2 * w - 4)
                    turn(2 * w - 3)
                if w >= 3:
                    weigh(w - 3)
            pe.wait_ge(w_made, C)
            pe.wait_ge(o_out, B)
            for i in range(C * NB):
                m, n = divmod(i, NB)
                if i >= 3:
                    pe.wait_ge(y_out, i - 2)
                for c in range(C):
                    last = M.matmul(bank[i % 3][:, :], w_res[:, c, P * m:P * m + P],
                                    o0[:, c, BB * n:BB * n + BB, :].rearrange("p b t -> p (b t)"),
                                    start=(c == 0), stop=(c == C - 1))
                last.then_inc(y_full, 1)

        @block.vector
        def _(dve):
            V = nc.vector
            for c in range(C):
                ws = w_res[:, c, :]
                V.tensor_copy(ws, g.w_out0[:, c, :]).then_inc(w_copied, 1)
                dve.wait_ge(w_copied, c + 1)
                sl = slice(P * c, P * c + P)
                V.tensor_tensor(w_res[:, c, sl], g.w_out0[:, c, sl], g.ident[:, :], ADD).then_inc(w_made, 1)
            dve.wait_ge(ada_full, 1)
            for m in range(6 * C):
                one = 1.0 if m // C in (1, 4) else 0.0
                last = V.tensor_scalar(g.ada[:, m, :], bank[7][:, B * m:B * m + B],
                                       g.vec[:, V_ADAB + m:V_ADAB + m + 1], one, ADD, ADD)
            last.then_inc(ada_out, 1)

            def top(u):
                if u >= 4:
                    dve.wait_ge(p_ready, u - 3)
                V.tensor_reduce(neg_max[:, u % 4, :], bank[u % 4][:, :].rearrange("p (h k) -> p h k", h=4),
                                op=ALU.max, axis=AX_X, negate=True).then_inc(max_ready, 1)

            def turned(u):
                dve.wait_ge(t_full, u + 1)
                if u >= 4:
                    dve.wait_ge(o_full, u // 2 - 1)
                V.tensor_copy(probT[:, u % 4, :], bank[4 + u % 2][:, :]).then_inc(t_out, 1)

            def inverse(u):
                dve.wait_ge(p_ready, u + 1)
                if u >= 4:
                    dve.wait_ge(pn_ready, u - 3)
                V.reciprocal(inv[:, u % 4, :], sums[:, u % 4, :]).then_inc(inv_ready, 1)

            for w in range(U // 2 + 2):
                if w < U // 2:
                    dve.wait_ge(s_full, w + 1)
                    top(2 * w)
                    top(2 * w + 1)
                if w >= 2:
                    turned(2 * w - 4)
                if w < U // 2:
                    inverse(2 * w)
                if w >= 2:
                    turned(2 * w - 3)
                if w < U // 2:
                    inverse(2 * w + 1)
            for i in range(C * NB):
                m, n = divmod(i, NB)
                bs = slice(BB * n, BB * n + BB)
                dve.wait_ge(y_full, i + 1)
                V.tensor_tensor(g.x1[:, :, m, bs].rearrange("p t b -> p b t"),
                                bank[i % 3][:, :].rearrange("p (b t) -> p b t", b=BB),
                                g.xT[:, m, bs, :], ADD).then_inc(y_out, 1)

        @block.scalar
        def _(act):
            A = nc.scalar

            def out(b):
                act.wait_ge(o_full, 2 * b + 2)
                A.activation(o0[:, :, b, :], bank[6 + b % 2][:, 0:C * T].rearrange("p (c t) -> p c t", c=C),
                             ACT.Copy).then_inc(o_out, 1)

            for u in range(U):
                act.wait_ge(max_ready, u + 1)
                if u >= 6:
                    act.wait_ge(t_full, u - 5)
                if u >= 4:
                    act.wait_ge(inv_ready, u - 3)
                for i in range(4):
                    last = A.activation(prob[:, u % 6, i, :], bank[u % 4][:, T * i:T * i + T], ACT.Exp,
                                        bias=neg_max[:, u % 4, i:i + 1], accum_out=sums[:, u % 4, i:i + 1])
                last.then_inc(p_ready, 1)
                if u % 4 == 3 and u >= 11:
                    out(u // 4 - 2)
            out(B - 2)
            out(B - 1)
            act.wait_ge(bias_made, 1)
            for m in range(C):
                act.wait_ge(y_out, NB * (m + 1))
                A.activation(g.drive[:, 0:T, m, :], g.x1[:, :, m, :], ACT.Identity,
                             bias=g.drive_b[:, m:m + 1], scale=DT / 2)

        @block.gpsimd
        def _(pool):
            G = nc.gpsimd
            G.tensor_scalar(g.drive_b[:, :], g.vec[:, V_BIAS1:V_BIAS1 + C], DT / 2,
                            -ALPHA / BETA * DT / 2, MUL, ADD).then_inc(bias_made, 1)
            for u in range(U):
                pool.wait_ge(inv_ready, u + 1)
                G.tensor_tensor(prob[:, u % 6, :, :], prob[:, u % 6, :, :],
                                inv[:, u % 4, :].unsqueeze(2).broadcast_to([P, 4, T]), MUL).then_inc(pn_ready, 1)


def scan1(nc, ctx, a, g):
    sb = lambda name, shape, dt=F32: ctx.enter_context(nc.sbuf_tensor(name, shape, dt))
    sem = lambda name: ctx.enter_context(nc.semaphore(name))
    tile = lambda name: sb(name, [P, W1])[:, :]
    y, s2, s3, s4 = tile("s1_y"), tile("s1_s2"), tile("s1_s3"), tile("s1_s4")
    sq, cube, rest = tile("s1_sq"), tile("s1_cube"), tile("s1_rest")
    p_raw, p1, p2, p3, p4 = (tile(f"s1_p{i}") for i in range(5))
    m1, m2, m3, m4 = (tile(f"s1_m{i}") for i in range(1, 5))
    qd1, qd2, gmq, gmq3 = (tile(f"s1_{n}") for n in ("qd1", "qd2", "gmq", "gmq3"))
    base1, base2, base3, base4 = (tile(f"s1_base{i}") for i in range(1, 5))
    acc2, acc3, acc4 = (tile(f"s1_acc{i}") for i in range(2, 5))
    msum, msum2, msum3, psum, m3s, mscaled, pm = (tile(f"s1_ms{i}") for i in range(7))
    th_f = tile("s1_tanh")
    warm = sb("s1_warm", [P, 1])
    th_hi = sb("s1_tanh_hi", [P, W1], F16)
    th_lo = sb("s1_tanh_lo", [P, W1], F16)
    coupled = g.bank[0][:, 0:W1]
    s_ready = sem("s_ready")
    hi_ready, th_ready, lo_ready = sem("hi_ready"), sem("th_ready"), sem("lo_ready")
    coupled_ready = sem("coupled_ready")
    dve_done, pool_done = sem("dve_done"), sem("pool_done")
    lap_done, lap_go = sem("lap_done"), sem("lap_go")
    init = sem("init1")
    ND, NP = 30, 10
    M2_AT, M3_AT = 9, 16
    h = DT / 2
    laps = T // LAP
    trace = g.trace[:, :, :, :].rearrange("p t c b -> p (t c b)")
    drive = g.drive[:, :, :, :].rearrange("p t c b -> p (t c b)")

    def end_lap(eng, lap):
        eng.sem_inc(lap_done, 1)
        eng.wait_ge(lap_go, lap + 1)

    with nc.Block() as block:
        @block.sync
        def _(sp):
            with sp.Fori(0, laps) as lap:
                sp.wait_ge(lap_done, lap * 4 + 4)
                for s, n in ((s_ready, 4), (hi_ready, 4), (th_ready, 4), (lo_ready, 4),
                             (coupled_ready, 4), (dve_done, ND), (pool_done, NP)):
                    sp.sem_inc(s, -n * LAP)
                sp.sem_inc(lap_go, 1)

        @block.vector
        def _(dve):
            V = nc.vector
            STT = V.scalar_tensor_tensor
            V.tensor_copy(y, g.condT[:, :, :].rearrange("p c b -> p (c b)")).then_inc(init, 1)
            V.tensor_scalar(p_raw, g.condT[:, :, :].rearrange("p c b -> p (c b)"), -ALPHA / BETA,
                            None, ADD).then_inc(init, 1)
            V.memset(drive[:, T * W1:], 0.0).then_inc(init, 1)

            def clip_p(do):
                return do(V.tensor_scalar(p1, p_raw, CLAMP - ALPHA / BETA, -CLAMP - ALPHA / BETA, ALU.min, ALU.max))

            dve.wait_ge(init, 3)
            V.tensor_copy(p1, p_raw).then_inc(init, 1)
            V.tensor_copy(trace[:, 0:W1], y).then_inc(init, 1)
            dve.wait_ge(init, 5)
            STT(pm, p1, -h, drive[:, 0:W1], MUL, ADD).then_inc(init, 1)
            dve.wait_ge(init, 6)
            dve.sem_inc(s_ready, 1)
            with dve.Fori(0, laps) as lap:
                for j in range(LAP):
                    done = [ND * j]

                    def do(ins):
                        ins.then_inc(dve_done, 1)
                        done[0] += 1
                        return done[0]

                    def after(n):
                        dve.wait_ge(dve_done, n)

                    def low(stage):
                        dve.wait_ge(th_ready, 4 * j + stage)
                        V.tensor_tensor(th_lo[:, :], th_f, th_hi[:, :], SUB).then_inc(lo_ready, 1)

                    def advance(stage, out, scale, n):
                        dve.wait_ge(coupled_ready, 4 * j + stage)
                        after(n)
                        STT(out, coupled, g.coup_scale[:, scale:scale + 1], rest, MUL, ADD).then_inc(s_ready, 1)

                    def stage_input(stage):
                        dve.wait_ge(s_ready, 4 * j + stage)

                    q = trace[:, bass.ds(lap * (LAP * W1) + W1 * j, W1)]
                    if j:
                        after(ND * j)
                    ns = do(V.tensor_tensor(sq, q, q, MUL))
                    do(V.tensor_tensor(base1, pm, q, ADD))
                    low(1)
                    after(ns)
                    nc_ = do(STT(cube, sq, -3.0, q, ADD, MUL))
                    nm = do(STT(m1, p1, -BETA, q, MUL, ADD))
                    after(nc_)
                    nr = do(STT(rest, cube, -h / 3, base1, MUL, ADD))
                    after(nm)
                    n = do(STT(p2, m1, h * EPSILON, p1, MUL, ADD))
                    advance(1, s2, 0, nr)
                    after(n)
                    dve.wait_ge(pool_done, NP * j + 1)
                    do(STT(base2, p2, -h, qd1, MUL, ADD))
                    stage_input(2)
                    ns = do(V.tensor_tensor(sq, s2, s2, MUL))
                    nm = do(STT(m2, p2, -BETA, s2, MUL, ADD))
                    assert nm == ND * j + M2_AT
                    after(ns)
                    nc_ = do(STT(cube, sq, -3.0, s2, ADD, MUL))
                    low(2)
                    after(nm)
                    n = do(STT(p3, m2, h * EPSILON, p1, MUL, ADD))
                    after(nc_)
                    nr = do(STT(rest, cube, -h / 3, base2, MUL, ADD))
                    after(n)
                    dve.wait_ge(pool_done, NP * j + 2)
                    do(STT(base3, p3, -DT, qd2, MUL, ADD))
                    advance(2, s3, 0, nr)
                    dve.wait_ge(pool_done, NP * j + 4)
                    do(STT(acc2, s2, 1 / 3, gmq3, MUL, ADD))
                    stage_input(3)
                    ns = do(V.tensor_tensor(sq, s3, s3, MUL))
                    nm = do(STT(m3, p3, -BETA, s3, MUL, ADD))
                    assert nm == ND * j + M3_AT
                    after(ns)
                    nc_ = do(STT(cube, sq, -3.0, s3, ADD, MUL))
                    low(3)
                    do(STT(acc3, s3, 2 / 3, acc2, MUL, ADD))
                    after(nc_)
                    nr = do(STT(rest, cube, -DT / 3, base3, MUL, ADD))
                    n = do(STT(p4, m3, DT * EPSILON, p1, MUL, ADD))
                    advance(3, s4, 1, nr)
                    after(n)
                    na = do(STT(acc4, p4, -h / 3, acc3, MUL, ADD))
                    stage_input(4)
                    ns = do(V.tensor_tensor(sq, s4, s4, MUL))
                    do(STT(m4, p4, -BETA, s4, MUL, ADD))
                    after(na)
                    do(STT(base4, s4, 1 / 3, acc4, MUL, ADD))
                    after(ns)
                    nc_ = do(STT(cube, sq, -3.0, s4, ADD, MUL))
                    low(4)
                    after(nc_)
                    nr = do(STT(rest, cube, -DT / 18, base4, MUL, ADD))
                    dve.wait_ge(pool_done, NP * j + NP)
                    n = do(STT(p_raw, m4, DT * EPSILON / 6, mscaled, MUL, ADD))
                    after(n)
                    n = clip_p(do)
                    advance(4, y, 2, nr)
                    after(n)
                    do(STT(pm, p1, -h, drive[:, bass.ds(lap * (LAP * W1) + W1 * (j + 1), W1)], MUL, ADD))
                    stage_input(5)
                    do(V.tensor_scalar(trace[:, bass.ds(lap * (LAP * W1) + W1 * (j + 1), W1)], y,
                                       CLAMP, -CLAMP, ALU.min, ALU.max))
                    assert done[0] == ND * j + ND, done[0]
                dve.wait_ge(s_ready, 4 * LAP + 1)
                dve.wait_ge(dve_done, ND * LAP)
                end_lap(dve, lap)
            for c in range(C):
                V.tensor_tensor(g.x2[:, c, :, :], g.x1[:, :, c, :].rearrange("p t b -> p b t"),
                                g.trace[:, 1:T + 1, c, :].rearrange("p t b -> p b t"), ADD)

        @block.gpsimd
        def _(pool):
            G = nc.gpsimd
            pool.wait_ge(init, 6)
            with pool.Fori(0, laps) as lap:
                for j in range(LAP):
                    q = trace[:, bass.ds(lap * (LAP * W1) + W1 * j, W1)]
                    gh = drive[:, bass.ds(lap * (LAP * W1) + W1 * j, W1)]
                    done = [NP * j]

                    def do(ins, wait=True):
                        ins.then_inc(pool_done, 1)
                        done[0] += 1
                        if wait:
                            pool.wait_ge(pool_done, done[0])

                    if j:
                        pool.wait_ge(dve_done, ND * j)
                    do(G.tensor_tensor(qd1, gh, q, ADD))
                    do(G.tensor_tensor(qd2, qd1, gh, ADD), False)
                    do(G.tensor_tensor(gmq, gh, q, SUB))
                    do(G.tensor_scalar(gmq3, gmq, 1 / 3, None, MUL), False)
                    pool.wait_ge(dve_done, ND * j + M2_AT)
                    do(G.tensor_tensor(msum, m2, m2, ADD))
                    do(G.tensor_tensor(msum2, msum, m1, ADD))
                    do(G.tensor_scalar(msum3, msum2, DT * EPSILON / 6, None, MUL))
                    do(G.tensor_tensor(psum, msum3, p1, ADD), False)
                    pool.wait_ge(dve_done, ND * j + M3_AT)
                    do(G.tensor_scalar(m3s, m3, DT * EPSILON / 3, None, MUL))
                    do(G.tensor_tensor(mscaled, m3s, psum, ADD), False)
                end_lap(pool, lap)

        @block.scalar
        def _(act):
            A = nc.scalar
            A.activation(warm[:, :], g.eps6[:, :], ACT.Tanh)
            with act.Fori(0, laps) as lap:
                for j in range(LAP):
                    for i, s in enumerate((y, s2, s3, s4)):
                        act.wait_ge(s_ready, 4 * j + i + 1)
                        A.activation(th_hi[:, :], s, ACT.Tanh).then_inc(hi_ready, 1)
                        A.activation(th_f, s, ACT.Tanh).then_inc(th_ready, 1)
                end_lap(act, lap)

        @block.tensor
        def _(pe):
            def product(w, th, first, last):
                for c in range(C):
                    for m in range(C):
                        o = D * c + P * m
                        ins = nc.tensor.matmul(coupled[:, B * m:B * m + B], w[:, o:o + P],
                                               th[:, B * c:B * c + B], start=(first and c == 0 and m == 0),
                                               stop=(last and c == C - 1), skip_group_check=True)
                return ins

            with pe.Fori(0, laps) as lap:
                for i in range(4 * LAP):
                    pe.wait_ge(hi_ready, i + 1)
                    product(g.coup_hi, th_hi, True, False)
                    product(g.coup_lo, th_hi, False, False)
                    pe.wait_ge(lo_ready, i + 1)
                    product(g.coup_hi, th_lo, False, True).then_inc(coupled_ready, 1)
                end_lap(pe, lap)


def norm_split(nc, ctx, a, g, tag, scale, shift, xh, xl, loads):
    sb = lambda name, shape, dt=F32: ctx.enter_context(nc.sbuf_tensor(name + tag, shape, dt))
    sem = lambda name: ctx.enter_context(nc.semaphore(name + tag))
    xc = sb("centred", [P, C, NB, 512])
    square = sb("square", [P, C, 2, 512])
    log_var = sb("log_var", [P, 2, 512])
    rstd = sb("rstd", [P, 2, 512])
    mod = sb("modulated", [P, C, 2, 512])
    mean_full, xc_ready, sq_ready, var_full = sem("mean_full"), sem("xc_ready"), sem("sq_ready"), sem("var_full")
    log_ready, rstd_ready, xhat_ready = sem("log_ready"), sem("rstd_ready"), sem("xhat_ready")
    mod_ready = [sem("mod_ready0"), sem("mod_ready1")]
    hi_ready, lo_ready = sem("hi_ready"), sem("lo_ready")
    bank = g.bank
    x2 = g.x2[:, :, :, :].rearrange("p c b t -> p c (b t)")
    blk = lambda n: slice(512 * n, 512 * n + 512)

    def modulate(eng, c, sem_done):
        for n in range(NB):
            eng.wait_ge(xhat_ready, C * n + c + 1)
            if n >= 2:
                eng.wait_ge(lo_ready, C * (n - 2) + c + 1)
            for i in range(BB):
                b = BB * n + i
                last = eng.tensor_scalar(mod[:, c, n % 2, T * i:T * i + T], xc[:, c, n, T * i:T * i + T],
                                         g.ada[:, C * scale + c, b:b + 1], g.ada[:, C * shift + c, b:b + 1],
                                         MUL, ADD)
            last.then_inc(sem_done, 1)
            yield n

    with nc.Block() as block:
        @block.sync
        def _(sp):
            loads(sp)

        @block.tensor
        def _(pe):
            M = nc.tensor
            for n in range(NB):
                for c in range(C):
                    last = M.matmul(bank[n][:, :], g.mean_w[:, :], x2[:, c, blk(n)], start=(c == 0),
                                    stop=(c == C - 1))
                last.then_inc(mean_full, 1)
            for n in range(NB):
                pe.wait_ge(sq_ready, C * n + C)
                for c in range(C):
                    last = M.matmul(bank[4 + n][:, :], g.mean_w[:, :], square[:, c, n % 2, :],
                                    start=(c == 0), stop=(c == C - 1))
                last.then_inc(var_full, 1)

        @block.vector
        def _(dve):
            V = nc.vector
            for n in range(NB):
                dve.wait_ge(mean_full, n + 1)
                for c in range(C):
                    V.tensor_tensor(xc[:, c, n, :], x2[:, c, blk(n)], bank[n][:, :], SUB).then_inc(xc_ready, 1)

            def low(n):
                for c in range(C):
                    dve.wait_ge(hi_ready, C * n + c + 1)
                    V.tensor_tensor(xl[:, c, blk(n)], mod[:, c, n % 2, :], xh[:, c, blk(n)].bitcast(F32),
                                    SUB).then_inc(lo_ready, 1)

            chunk0 = modulate(dve, 0, mod_ready[0])
            for n in range(NB):
                dve.wait_ge(rstd_ready, n + 1)
                dve.wait_ge(sq_ready, C * n + C)
                for c in range(C):
                    V.tensor_tensor(xc[:, c, n, :], xc[:, c, n, :], rstd[:, n % 2, :], MUL).then_inc(xhat_ready, 1)
                next(chunk0)
                if n:
                    low(n - 1)
            low(NB - 1)

        @block.gpsimd
        def _(pool):
            for n in modulate(pool, 1, mod_ready[1]):
                pass

        @block.scalar
        def _(act):
            A = nc.scalar

            def squares(n):
                for c in range(C):
                    act.wait_ge(xc_ready, C * n + c + 1)
                    if n >= 2:
                        act.wait_ge(var_full, n - 1)
                    A.activation(square[:, c, n % 2, :], xc[:, c, n, :], ACT.Square).then_inc(sq_ready, 1)

            def high(n):
                for c in range(C):
                    act.wait_ge(mod_ready[c], n + 1)
                    A.activation(xh[:, c, blk(n)], mod[:, c, n % 2, :], ACT.Copy).then_inc(hi_ready, 1)

            for n in range(0, NB, 2):
                squares(n)
                squares(n + 1)
                for i in range(2):
                    act.wait_ge(var_full, n + i + 1)
                    A.activation(log_var[:, i, :], bank[4 + n + i][:, :], ACT.Ln, bias=g.eps6[:, :]).then_inc(log_ready, 1)
                for i in range(2):
                    act.wait_ge(log_ready, n + i + 1)
                    if n:
                        act.wait_ge(xhat_ready, C * (n + i - 1))
                    A.activation(rstd[:, i, :], log_var[:, i, :], ACT.Exp, scale=-0.5).then_inc(rstd_ready, 1)
                if n:
                    high(n - 2)
                    high(n - 1)
            high(NB - 2)
            high(NB - 1)


def attend2(nc, ctx, a, g, xh, xl):
    sb = lambda name, shape, dt=F32: ctx.enter_context(nc.sbuf_tensor(name, shape, dt))
    sem = lambda name: ctx.enter_context(nc.semaphore(name))
    HG, UNITS, GROUPS, INNER = 4, 16, 64, H2 * D2
    w_h = sb("w2_hi", [P, 3, C, 512], F32R)
    w_l = sb("w2_lo", [P, 3, C, 512], F32R)
    w_stage = g.w_stage
    ow_stage = g.ow_stage
    ow_h = sb("ow_hi", [P, HG, D], F32R)
    ow_l = sb("ow_lo", [P, HG, D], F32R)
    o_h = sb("o2_hi", [P, 2, HG, 512], F32R)
    o_l = sb("o2_lo", [P, 2, HG, 512], F32R)
    q2 = sb("q2", [P, 2, HG, 512])
    k2 = sb("k2", [P, 2, HG, 512])
    v2 = sb("v2", [P, 2, BB, 512])
    prob = sb("prob2", [P, 2, HG, T])
    probT = sb("probT2", [P, 2, 512])
    neg_max = sb("neg_max2", [P, 2, HG])
    sums = sb("sums2", [P, 2, HG])
    inv = sb("inv2", [P, 2, HG])
    q_bias = sb("q_bias", [P, H2])
    gate_b = sb("gate_b", [P, C, B])
    wh_ready, wl_ready = sem("wh_ready"), sem("wl_ready")
    owh_ready, owl_ready = sem("owh_ready"), sem("owl_ready")
    proj_full, q_out, kv_out = sem("proj_full"), sem("q_out"), sem("kv_out")
    s_full, max_ready, p_ready, inv_ready, pn_ready = (
        sem("s_full2"), sem("max_ready2"), sem("p_ready2"), sem("inv_ready2"), sem("pn_ready2"))
    t_full, t_out, o_full, oh_ready, ol_ready = (
        sem("t_full2"), sem("t_out2"), sem("o_full2"), sem("oh_ready2"), sem("ol_ready2"))
    y_full, y_out = sem("y_full2"), sem("y_out2")
    small_made, base_made = sem("small_made2"), sem("base_made2")
    bank = g.bank
    STEPS = 12
    evac_steps = {}

    def proj_evacuated(eng, i):
        u, s = divmod(i, STEPS)
        if s < 4:
            eng.wait_ge(q_out, 4 * u + s + 1)
        else:
            eng.wait_ge(kv_out, 8 * u + s - 3)

    def slots():
        for p in range(UNITS + 2):
            for k in range(4):
                yield p, k, 4 * (p - 1) + k

    with nc.Block() as block:
        @block.sync
        def _(sp):
            for hg in range(1, HG):
                sp.wait_ge(wl_ready, 3 * hg)
                load_w2(sp, a, g, hg)
                sp.wait_ge(owl_ready, hg)
                load_ow(sp, a, g, hg)
                if hg >= 2:
                    sp.wait_ge(kv_out, 8 * 4 * (hg - 1))
                load_vb(sp, a, g, hg)

        @block.tensor
        def _(pe):
            M = nc.tensor

            def three(out, parts, last_of):
                n = 0
                for sh, sl, mh, ml in parts:
                    for s, m in ((sh, mh), (sh, ml), (sl, mh)):
                        ins = M.matmul(out, s, m, start=(n == 0), stop=(n == 3 * len(parts) - 1))
                        n += 1
                ins.then_inc(last_of, 1)

            def project(i):
                u, s = divmod(i, STEPS)
                hg, bg = divmod(u, 4)
                w, j = divmod(s, 4)
                pe.wait_ge(wl_ready, 3 * hg + w + 1)
                if i >= 2:
                    proj_evacuated(pe, i - 2)
                parts = []
                for c in range(C):
                    if w < 2:
                        cols, toks = slice(D2 * j, D2 * j + D2), slice(512 * bg, 512 * bg + 512)
                        parts.append((w_h[:, w, c, cols], w_l[:, w, c, cols], xh[:, c, toks], xl[:, c, toks]))
                    else:
                        t0 = 512 * bg + T * j
                        parts.append((xh[:, c, t0:t0 + T], xl[:, c, t0:t0 + T], w_h[:, w, c, :], w_l[:, w, c, :]))
                three(bank[i % 2][:, :], parts, proj_full)

            for p, k, grp in slots():
                if 0 <= grp < GROUPS:
                    u = p - 1
                    pe.wait_ge(q_out, 4 * u + 4)
                    pe.wait_ge(kv_out, 8 * u + 4)
                    if grp >= 2:
                        pe.wait_ge(p_ready, grp - 1)
                    ts = slice(T * k, T * k + T)
                    for h in range(HG):
                        last = M.matmul(bank[2 + grp % 2][:, T * h:T * h + T], q2[:, u % 2, h, ts],
                                        k2[:, u % 2, h, ts], start=True, stop=True)
                    last.then_inc(s_full, 1)
                i = STEPS * p + 3 * k
                if p < UNITS:
                    project(i)
                if 0 <= grp - 1 < GROUPS:
                    v = grp - 1
                    pe.wait_ge(pn_ready, v + 1)
                    if v >= 2:
                        pe.wait_ge(t_out, v - 1)
                    for h in range(HG):
                        last = M.transpose(bank[4 + v % 2][:, T * h:T * h + T], prob[:, v % 2, h, :], g.ident[:, :])
                    last.then_inc(t_full, 1)
                if p < UNITS:
                    project(i + 1)
                if 0 <= grp - 2 < GROUPS:
                    v = grp - 2
                    u, b = divmod(v, 4)
                    pe.wait_ge(kv_out, 8 * u + 8)
                    pe.wait_ge(t_out, v + 1)
                    pe.wait_ge(ol_ready, v)
                    for h in range(HG):
                        last = M.matmul(bank[6][:, T * h:T * h + T], v2[:, u % 2, b, D2 * h:D2 * h + D2],
                                        probT[:, v % 2, T * h:T * h + T], start=True, stop=True)
                    last.then_inc(o_full, 1)
                if p < UNITS:
                    project(i + 2)
                if p >= 2 and k >= 2:
                    u, m = p - 2, k - 2
                    pe.wait_ge(ol_ready, 4 * u + 4)
                    pe.wait_ge(owl_ready, u // 4 + 1)
                    if 2 * u + m:
                        pe.wait_ge(y_out, 2 * u + m)
                    ms = slice(P * m, P * m + P)
                    three(bank[7][:, :], [(ow_h[:, h, ms], ow_l[:, h, ms], o_h[:, u % 2, h, :],
                                           o_l[:, u % 2, h, :]) for h in range(HG)], y_full)

        def conversions(p, k):
            if p % 4 == 3 and p < UNITS - 1 and k >= 2:
                yield "w", p // 4 + 1, k - 2
            if p % 4 == 0 and 4 <= p < UNITS and k == 0:
                yield "w", p // 4, 2
            if p % 4 == 2 and 6 <= p < UNITS and k == 0:
                yield "ow", p // 4, 0

        first = [("w", 0, 0), ("w", 0, 1), ("w", 0, 2), ("ow", 0, 0)]

        @block.scalar
        def _(act):
            A = nc.scalar

            def convert(what, hg, part):
                if what == "w":
                    act.wait_ge(g.d_w2, 48 * (hg + 1))
                    if hg:
                        act.wait_ge(proj_full, STEPS * (4 * hg - 1) + 4 * part + 4)
                    for c in range(C):
                        A.activation(w_h[:, part, c, :], w_stage[:, part, c, :], ACT.Copy).then_inc(wh_ready, 1)
                else:
                    act.wait_ge(g.d_ow, 16 * (hg + 1))
                    if hg:
                        act.wait_ge(y_full, 2 * 4 * hg)
                    for c in range(2):
                        A.activation(ow_h[:, 2 * c:2 * c + 2, :], ow_stage[:, 2 * c:2 * c + 2, :],
                                     ACT.Copy).then_inc(owh_ready, 1)

            for item in first:
                convert(*item)
            act.wait_ge(small_made, 1)
            for p, k, grp in slots():
                for item in conversions(p, k):
                    convert(*item)
                if 0 <= grp < GROUPS:
                    act.wait_ge(max_ready, grp + 1)
                    if grp >= 2:
                        act.wait_ge(t_full, grp - 1)
                        act.wait_ge(inv_ready, grp - 1)
                    for h in range(HG):
                        last = A.activation(prob[:, grp % 2, h, :], bank[2 + grp % 2][:, T * h:T * h + T], ACT.Exp,
                                            bias=neg_max[:, grp % 2, h:h + 1], accum_out=sums[:, grp % 2, h:h + 1])
                    last.then_inc(p_ready, 1)
                for i in range(STEPS * p + 3 * k, STEPS * p + 3 * k + 3):
                    u, s = divmod(i, STEPS)
                    if p < UNITS and s < 4:
                        act.wait_ge(proj_full, i + 1)
                        if u >= 2:
                            act.wait_ge(s_full, 4 * (u - 1))
                        h = HG * (u // 4) + s
                        A.activation(q2[:, u % 2, s, :], bank[i % 2][:, :], ACT.Identity,
                                     bias=q_bias[:, h:h + 1], scale=D2 ** -0.5).then_inc(q_out, 1)
                if 0 <= grp - 2 < GROUPS:
                    v = grp - 2
                    u, b = divmod(v, 4)
                    act.wait_ge(o_full, v + 1)
                    if u >= 2:
                        act.wait_ge(y_full, 2 * (u - 1))
                    A.activation(o_h[:, u % 2, :, T * b:T * b + T],
                                 bank[6][:, :].rearrange("p (h t) -> p h t", h=HG), ACT.Copy).then_inc(oh_ready, 1)

        @block.vector
        def _(dve):
            V = nc.vector

            def convert(what, hg, part):
                if what == "w":
                    for c in range(C):
                        dve.wait_ge(wh_ready, C * (3 * hg + part) + c + 1)
                        last = V.tensor_tensor(w_l[:, part, c, :], w_stage[:, part, c, :],
                                               w_h[:, part, c, :].bitcast(F32), SUB)
                    last.then_inc(wl_ready, 1)
                else:
                    for c in range(2):
                        dve.wait_ge(owh_ready, 2 * hg + c + 1)
                        hs = slice(2 * c, 2 * c + 2)
                        last = V.tensor_tensor(ow_l[:, hs, :], ow_stage[:, hs, :], ow_h[:, hs, :].bitcast(F32), SUB)
                    last.then_inc(owl_ready, 1)

            V.tensor_scalar(q_bias[:, :], g.vec[:, V_QKB:V_QKB + H2], D2 ** -0.5, None, MUL).then_inc(small_made, 1)
            for item in first:
                convert(*item)
            for p, k, grp in slots():
                for item in conversions(p, k):
                    convert(*item)
                if 0 <= grp < GROUPS:
                    dve.wait_ge(s_full, grp + 1)
                    if grp >= 2:
                        dve.wait_ge(p_ready, grp - 1)
                    V.tensor_reduce(neg_max[:, grp % 2, :], bank[2 + grp % 2][:, :].rearrange("p (h k) -> p h k", h=HG),
                                    op=ALU.max, axis=AX_X, negate=True).then_inc(max_ready, 1)

                def out(i):
                    u, s = divmod(i, STEPS)
                    if p >= UNITS or s < 4:
                        return
                    dve.wait_ge(proj_full, i + 1)
                    if s < 8:
                        if u >= 2:
                            dve.wait_ge(s_full, 4 * (u - 1))
                        bias = g.vec[:, V_QKB + H2 + HG * (u // 4) + s - 4:][:, 0:1]
                        V.tensor_scalar(k2[:, u % 2, s - 4, :], bank[i % 2][:, :], bias, None, ADD).then_inc(kv_out, 1)
                    else:
                        dve.wait_ge(g.d_vb[u // 4], 16)
                        if u >= 2:
                            dve.wait_ge(o_full, 4 * (u - 1))
                        V.tensor_tensor(v2[:, u % 2, s - 8, :], bank[i % 2][:, :], g.v_bias[:, (u // 4) % 2, :],
                                        ADD).then_inc(kv_out, 1)

                out(STEPS * p + 3 * k)
                if 0 <= grp - 1 < GROUPS:
                    v = grp - 1
                    dve.wait_ge(t_full, v + 1)
                    if v >= 2:
                        dve.wait_ge(o_full, v - 1)
                    V.tensor_copy(probT[:, v % 2, :], bank[4 + v % 2][:, :]).then_inc(t_out, 1)
                if 0 <= grp < GROUPS:
                    dve.wait_ge(p_ready, grp + 1)
                    if grp >= 2:
                        dve.wait_ge(pn_ready, grp - 1)
                    V.reciprocal(inv[:, grp % 2, :], sums[:, grp % 2, :]).then_inc(inv_ready, 1)
                out(STEPS * p + 3 * k + 1)
                if 0 <= grp - 2 < GROUPS:
                    v = grp - 2
                    u, b = divmod(v, 4)
                    dve.wait_ge(oh_ready, v + 1)
                    V.tensor_tensor(o_l[:, u % 2, :, T * b:T * b + T],
                                    bank[6][:, :].rearrange("p (h t) -> p h t", h=HG),
                                    o_h[:, u % 2, :, T * b:T * b + T].bitcast(F32), SUB).then_inc(ol_ready, 1)
                out(STEPS * p + 3 * k + 2)
                if p >= 2 and k >= 2:
                    u, m = p - 2, k - 2
                    dve.wait_ge(y_full, 2 * u + m + 1)
                    dve.wait_ge(base_made, C)
                    if u >= 4:
                        dve.wait_ge(y_out, 2 * (u - 4) + m + 1)
                    for i in range(BB):
                        b = BB * (u % 4) + i
                        last = V.scalar_tensor_tensor(g.x2[:, m, b, :], bank[7][:, T * i:T * i + T],
                                                      g.ada[:, 2 * C + m, b:b + 1], g.x2[:, m, b, :], MUL, ADD)
                    last.then_inc(y_out, 1)

        @block.gpsimd
        def _(pool):
            G = nc.gpsimd
            for c in range(C):
                G.tensor_scalar(gate_b[:, c, :], g.ada[:, 2 * C + c, :], g.vec[:, V_OUTB + c:V_OUTB + c + 1],
                                None, MUL).then_inc(small_made, 1)
            pool.wait_ge(small_made, 1 + C)
            for c in range(C):
                G.tensor_tensor(g.x2[:, c, :, :], g.x2[:, c, :, :],
                                gate_b[:, c, :].unsqueeze(2).broadcast_to([P, B, T]), ADD).then_inc(base_made, 1)
            for grp in range(GROUPS):
                pool.wait_ge(inv_ready, grp + 1)
                G.tensor_tensor(prob[:, grp % 2, :, :], prob[:, grp % 2, :, :],
                                inv[:, grp % 2, :].unsqueeze(2).broadcast_to([P, HG, T]), MUL).then_inc(pn_ready, 1)


def load_w2(sp, a, g, hg):
    w = a["L2_cond_qkv_w"].rearrange("(c p) n -> p c n", p=P)
    for part in range(3):
        o = H2 * D2 * part + 512 * hg
        sp.dma_start(g.w_stage[:, part, :, :], w[:, :, o:o + 512]).then_inc(g.d_w2, 16)


def load_ow(sp, a, g, hg):
    w = a["L2_cond_out_w"][512 * hg:512 * hg + 512, :].rearrange("(h p) n -> p h n", p=P)
    sp.dma_start(g.ow_stage[:, :, :], w).then_inc(g.d_ow, 16)


def load_vb(sp, a, g, hg):
    o = 2 * H2 * D2 + 512 * hg
    sp.dma_start(g.v_bias[:, hg % 2, :], a["L2_cond_qkv_b"][o:o + 512].partition_broadcast(P)).then_inc(g.d_vb[hg], 16)


def feed_forward(nc, ctx, a, g, xh, xl, x3_dram):
    sb = lambda name, shape, dt=F32: ctx.enter_context(nc.sbuf_tensor(name, shape, dt))
    sem = lambda name: ctx.enter_context(nc.semaphore(name))
    M1 = FF // P
    w1_h, w1_l = sb("w1_hi", [P, C, FF], F32R), sb("w1_lo", [P, C, FF], F32R)
    w2_h, w2_l = sb("ffw2_hi", [P, M1, D], F32R), sb("ffw2_lo", [P, M1, D], F32R)
    act_f = sb("gelu", [P, 4, 512])
    h_h, h_l = sb("hidden_hi", [P, M1, 512], F32R), sb("hidden_lo", [P, M1, 512], F32R)
    x3_tok = g.w1_stage[:, 0, :].rearrange("p (i b f) -> p i b f", i=2, b=2)
    wh_ready, wl_ready = sem("ffwh_ready"), sem("ffwl_ready")
    f_full, gelu_ready, hh_ready, hl_ready = sem("f_full"), sem("gelu_ready"), sem("hh_ready"), sem("hl_ready")
    y_full, y_out, with_b = sem("fy_full"), sem("fy_out"), sem("with_b")
    t_full, t_out = sem("x3t_full"), sem("x3t_out")
    gate_b, gb_made = sb("gate_b2", [P, C, B]), sem("gb_made")
    doubled = sem("doubled")
    bank = g.bank
    pieces = [(g.w1_stage[:, c, o:o + 512], w1_h[:, c, o:o + 512], w1_l[:, c, o:o + 512])
              for o in (0, 512) for c in range(C)]
    pieces += [(g.ffw2_stage[:, k:k + 2, :], w2_h[:, k:k + 2, :], w2_l[:, k:k + 2, :]) for k in range(0, M1, 2)]

    with nc.Block() as block:
        @block.tensor
        def _(pe):
            M = nc.tensor

            def three(out, parts, full):
                n = 0
                for sh, sl, mh, ml in parts:
                    for s, m in ((sh, mh), (sh, ml), (sl, mh)):
                        ins = M.matmul(out, s, m, start=(n == 0), stop=(n == 3 * len(parts) - 1))
                        n += 1
                ins.then_inc(full, 1)

            def turn(n):
                pe.wait_ge(y_out, C * n + C)
                for i in range(2):
                    s = 2 * n + i
                    if s >= 2:
                        pe.wait_ge(t_out, s - 1)
                    for k in range(2):
                        for c in range(C):
                            last = M.transpose(bank[6 + i][:, D * k + P * c:D * k + P * c + P],
                                               g.x2[:, c, 2 * s + k, :], g.ident[:, :])
                    last.then_inc(t_full, 1)

            for n in range(NB):
                toks = slice(512 * n, 512 * n + 512)
                for m in range(M1):
                    if n == 0:
                        pe.wait_ge(wl_ready, 2 * (m // 4) + 2)
                    s = M1 * n + m
                    if s >= 4:
                        pe.wait_ge(gelu_ready, s - 3)
                    ms = slice(P * m, P * m + P)
                    three(bank[s % 4][:, :], [(w1_h[:, c, ms], w1_l[:, c, ms], xh[:, c, toks], xl[:, c, toks])
                                              for c in range(C)], f_full)
                if n:
                    turn(n - 1)
                pe.wait_ge(wl_ready, 8)
                pe.wait_ge(hl_ready, M1 * n + M1)
                for m in range(C):
                    s = C * n + m
                    if s >= 2:
                        pe.wait_ge(y_out, s - 1)
                    ms = slice(P * m, P * m + P)
                    three(bank[4 + m][:, :], [(w2_h[:, k, ms], w2_l[:, k, ms], h_h[:, k, :], h_l[:, k, :])
                                              for k in range(M1)], y_full)
            turn(NB - 1)

        @block.scalar
        def _(act):
            A = nc.scalar
            act.wait_ge(g.d_ff, 32)
            for i, (stage, hi, lo) in enumerate(pieces):
                A.activation(hi, stage, ACT.Copy).then_inc(wh_ready, 1)

            def gelu(s):
                act.wait_ge(f_full, s + 1)
                if s >= 4:
                    act.wait_ge(hl_ready, s - 3)
                A.activation(act_f[:, s % 4, :], bank[s % 4][:, :], ACT.Gelu,
                             bias=g.vec[:, V_B1 + s % M1:V_B1 + s % M1 + 1]).then_inc(gelu_ready, 1)

            def high(s):
                n, m = divmod(s, M1)
                act.wait_ge(gelu_ready, s + 1)
                if n:
                    act.wait_ge(y_full, C * n)
                A.activation(h_h[:, m, :], act_f[:, s % 4, :], ACT.Copy).then_inc(hh_ready, 1)

            for n in range(NB):
                gelu(M1 * n)
                for m in range(1, M1):
                    gelu(M1 * n + m)
                    high(M1 * n + m - 1)
                high(M1 * n + M1 - 1)

        @block.vector
        def _(dve):
            V = nc.vector
            for i, (stage, hi, lo) in enumerate(pieces):
                dve.wait_ge(wh_ready, i + 1)
                V.tensor_tensor(lo, stage, hi.bitcast(F32), SUB).then_inc(wl_ready, 1)

            def tokens_out(n):
                for i in range(2):
                    s = 2 * n + i
                    dve.wait_ge(t_full, s + 1)
                    if s >= 2:
                        dve.wait_ge(g.d_x3[i], 16 * (s // 2))
                    V.tensor_copy(x3_tok[:, i, :, :], bank[6 + i][:, :].rearrange("p (b f) -> p b f", b=2)).then_inc(t_out, 1)

            for n in range(NB):
                for m in range(M1):
                    s = M1 * n + m
                    dve.wait_ge(hh_ready, s + 1)
                    V.tensor_tensor(h_l[:, m, :], act_f[:, s % 4, :], h_h[:, m, :].bitcast(F32),
                                    SUB).then_inc(hl_ready, 1)
                if n:
                    tokens_out(n - 1)
                for m in range(C):
                    s = C * n + m
                    dve.wait_ge(y_full, s + 1)
                    dve.wait_ge(with_b, m + 1)
                    for i in range(BB):
                        b = BB * n + i
                        last = V.scalar_tensor_tensor(g.x2[:, m, b, :], bank[4 + m][:, T * i:T * i + T],
                                                      g.ada[:, 5 * C + m, b:b + 1], g.x2[:, m, b, :], MUL, ADD)
                    last.then_inc(y_out, 1)
            tokens_out(NB - 1)

        @block.gpsimd
        def _(pool):
            G = nc.gpsimd
            G.memset(g.bias3[:, :, :], 0.0).then_inc(g.zeroed3, 1)
            G.memset(g.h[0][:, :], 0.0).then_inc(g.zeroed3, 1)
            pool.wait_ge(g.d_keep, 32)
            for c in range(C):
                G.tensor_tensor(g.x2[:, c, :, :], g.x2[:, c, :, :], g.x2_in[:, c, :, :], ADD).then_inc(doubled, 1)
                G.tensor_scalar(gate_b[:, c, :], g.ada[:, 5 * C + c, :], g.vec[:, V_B2 + c:V_B2 + c + 1],
                                None, MUL).then_inc(gb_made, 1)
                pool.wait_ge(gb_made, c + 1)
                pool.wait_ge(doubled, c + 1)
                G.tensor_tensor(g.x2[:, c, :, :], g.x2[:, c, :, :],
                                gate_b[:, c, :].unsqueeze(2).broadcast_to([P, B, T]), ADD).then_inc(with_b, 1)
            gru_zeros(nc, g)

        @block.sync
        def _(sp):
            gru_loads(sp, a, g)
            for s in range(2 * NB):
                sp.wait_ge(t_out, s + 1)
                sp.dma_start(x3_dram[2 * s:2 * s + 2, :, :].rearrange("b t f -> t b f"),
                             x3_tok[:, s % 2, :, :]).then_inc(g.d_x3[s % 2], 16)
            for i in range(2):
                sp.wait_ge(g.d_x3[i], 16 * NB)
            sp.wait_ge(g.d_gru, 16 * 13)


def gru(nc, ctx, a, g, out, x3_dram):
    sb = lambda name, shape, dt=F32: ctx.enter_context(nc.sbuf_tensor(name, shape, dt))
    sem = lambda name: ctx.enter_context(nc.semaphore(name))
    J, E = 4, D // 4
    x3s, w_x, w_h, bias, ones = g.x3s, g.w_x, g.w_h, g.bias3, g.ones3
    h, xcol = g.h, g.xcol
    hT = sb("hT", [P, C, 32])
    rz = sb("rz", [P, 2 * E])
    rhn, pre, cand, keep, zh, new = (sb(n, [P, E]) for n in ("rhn", "pre", "cand", "keep", "zh", "new"))
    warm = sb("warm3", [P, 1])
    d_first, d_rest = sem("d_x3s_first"), sem("d_x3s_rest")
    h_ready, hT_ready, g_full = sem("h_ready"), sem("hT_ready"), sem("g_full")
    xb_full = sem("xb_full")
    rz_ready, pre_ready, cand_ready = sem("rz_ready"), sem("pre_ready"), sem("cand_ready")
    x_ready, added = sem("xcol_ready"), sem("added")
    chain = sem("gru_chain")
    lap_done, lap_go, d_out = sem("lap_done3"), sem("lap_go3"), sem("d_out")
    NC = 4
    laps = T // LAP3
    bank = g.bank
    state = lambda d, j: d[:, :, E * j:E * j + E]

    def end_lap(eng, lap):
        eng.sem_inc(lap_done, 1)
        eng.wait_ge(lap_go, lap + 1)

    with nc.Block() as block:
        @block.sync
        def _(sp):
            for ts, d in ((slice(0, LAP3), d_first), (slice(LAP3, T), d_rest)):
                for j in range(J):
                    sp.dma_start(x3s[32 * j:32 * j + B, ts, :], state(x3_dram, j)[:, ts, :]).then_inc(d, 16)
            with sp.Fori(0, laps) as lap:
                sp.wait_ge(lap_done, lap * 4 + 4)
                sp.wait_ge(d_rest, 16 * J)
                for s, n in ((h_ready, 1), (hT_ready, 1), (g_full, 1), (xb_full, 1), (rz_ready, 1),
                             (pre_ready, 1), (cand_ready, 1), (x_ready, 1), (added, 1), (chain, NC)):
                    sp.sem_inc(s, -n * LAP3)
                sp.sem_inc(lap_go, 1)
                for j in range(J):
                    o = state(out, j)[:, bass.ds(lap * LAP3, LAP3), :]
                    sp.dma_start(o, x3s[32 * j:32 * j + B, bass.ds(lap * LAP3, LAP3), :]).then_inc(d_out, 16)
            sp.wait_ge(d_out, 16 * J * laps)

        @block.gpsimd
        def _(pool):
            G = nc.gpsimd
            x3 = g.x2[:, :, :, :]
            x3_next = g.x2_flat[:, LAP3:LAP3 + C * TOK].rearrange("p (c b t) -> p c b t", c=C, b=B)

            def column(half, x):
                G.tensor_copy(xcol[:, half, :, 0:B].unsqueeze(3), x).then_inc(x_ready, 1)

            column(0, x3[:, :, :, 0:1])
            pool.wait_ge(d_first, 16 * J)
            with pool.Fori(0, laps) as lap:
                for j in range(LAP3):
                    if j:
                        pool.wait_ge(xb_full, j)
                    if j + 1 < LAP3:
                        column((j + 1) % 2, x3[:, :, :, bass.ds(lap * LAP3 + j + 1, 1)])
                    else:
                        column(0, x3_next[:, :, :, bass.ds(lap * LAP3, 1)])
                    pool.wait_ge(h_ready, j + 2)
                    t = x3s[:, bass.ds(lap * LAP3 + j, 1), :].rearrange("p t e -> p (t e)")
                    G.tensor_tensor(t, t, h[(j + 1) % 2][:, :], ADD).then_inc(added, 1)
                pool.wait_ge(added, LAP3)
                pool.wait_ge(x_ready, LAP3 + 1)
                end_lap(pool, lap)

        @block.tensor
        def _(pe):
            M = nc.tensor
            def inputs(s):
                gates = lambda j, lo, n: bank[s % 2][32 * j:32 * j + 32, E * lo:E * lo + E * n].rearrange(
                    "p (g e) -> p g e", e=E)
                for j in range(J):
                    M.matmul(gates(j, 0, 4), ones[:, :], bias[:, :, E * j:E * j + E], start=True, stop=False,
                             skip_group_check=True)
                pe.wait_ge(x_ready, s + 1)
                for j in range(J):
                    for c in range(C):
                        last = M.matmul(gates(j, 0, 3), xcol[:, s % 2, c, :], w_x[:, c, :, E * j:E * j + E],
                                        start=False, stop=False, skip_group_check=True)
                last.then_inc(xb_full, 1)

            inputs(0)
            with pe.Fori(0, laps) as lap:
                for s in range(LAP3):
                    pe.wait_ge(hT_ready, s + 1)
                    for j in range(J):
                        for c in range(C):
                            o = bank[s % 2][32 * j:32 * j + 32, E:4 * E].rearrange("p (g e) -> p g e", e=E)
                            last = M.matmul(o, hT[:, c, :], w_h[:, c, :, E * j:E * j + E], start=False,
                                            stop=(c == C - 1), skip_group_check=True)
                    last.then_inc(g_full, 1)
                    if s:
                        pe.wait_ge(pre_ready, s)
                    inputs(s + 1)
                pe.wait_ge(xb_full, LAP3 + 1)
                end_lap(pe, lap)

        @block.scalar
        def _(act):
            A = nc.scalar
            A.activation(warm[:, :], g.eps6[:, :], ACT.Sigmoid)
            with act.Fori(0, laps) as lap:
                for s in range(LAP3):
                    act.wait_ge(g_full, s + 1)
                    A.activation(rz[:, :], bank[s % 2][:, E:3 * E], ACT.Sigmoid).then_inc(rz_ready, 1)
                    act.wait_ge(pre_ready, s + 1)
                    A.activation(cand[:, :], pre[:, :], ACT.Tanh).then_inc(cand_ready, 1)
                end_lap(act, lap)

        @block.vector
        def _(dve):
            V = nc.vector
            dve.sem_inc(h_ready, 1)
            with dve.Fori(0, laps) as lap:
                for s in range(LAP3):
                    def do(ins, n):
                        ins.then_inc(chain, 1)

                    n0 = NC * s
                    dve.wait_ge(h_ready, s + 1)
                    V.transpose(hT[:, :, :].rearrange("p c b -> p (c b)"), h[s % 2][:, :]).then_inc(hT_ready, 1)
                    dve.wait_ge(rz_ready, s + 1)
                    V.tensor_tensor(rhn[:, :], rz[:, 0:E], bank[s % 2][:, 3 * E:4 * E], MUL).then_inc(chain, 1)
                    dve.wait_ge(chain, n0 + 1)
                    V.tensor_tensor(pre[:, :], rhn[:, :], bank[s % 2][:, 0:E], ADD).then_inc(pre_ready, 1)
                    V.tensor_scalar(keep[:, :], rz[:, E:2 * E], -1.0, 1.0, MUL, ADD).then_inc(chain, 1)
                    V.tensor_tensor(zh[:, :], rz[:, E:2 * E], h[s % 2][:, :], MUL).then_inc(chain, 1)
                    dve.wait_ge(cand_ready, s + 1)
                    dve.wait_ge(chain, n0 + 3)
                    V.tensor_tensor(new[:, :], cand[:, :], keep[:, :], MUL).then_inc(chain, 1)
                    dve.wait_ge(chain, n0 + 4)
                    if s >= 2:
                        dve.wait_ge(added, s - 1)
                    V.tensor_tensor(h[(s + 1) % 2][:, :], new[:, :], zh[:, :], ADD).then_inc(h_ready, 1)
                dve.wait_ge(h_ready, LAP3 + 1)
                end_lap(dve, lap)


def gru_buffers(sb, g):
    E = D // 4
    g.w_x = sb("w_x", [P, C, 3, D])
    g.w_h = sb("w_h", [P, C, 3, D])
    g.bias3 = sb("bias3", [2, 4, D])
    g.ones3 = sb("ones3", [2, 32])
    g.h = [sb(f"h{i}", [P, E]) for i in range(2)]
    g.xcol = sb("xcol", [P, 2, C, 32])
    g.x3s = sb("x3s", [P, T, E])


def gru_zeros(nc, g):
    G = nc.gpsimd
    G.memset(g.ones3[:, :], 1.0)
    G.memset(g.h[1][:, :], 0.0)
    G.memset(g.xcol[:, :, :, :], 0.0)
    G.memset(g.x2_flat[:, C * TOK:], 0.0)
    G.memset(g.x3s[:, :, :], 0.0)


def gru_loads(sp, a, g):
    w_i = a["L3_cond_W_ih"].rearrange("(c p) n -> p c n", p=P)
    sp.dma_start(g.w_x[:, :, 0, :], w_i[:, :, 2 * D:]).then_inc(g.d_gru, 16)
    sp.dma_start(g.w_x[:, :, 1:3, :].rearrange("p c g n -> p c (g n)"), w_i[:, :, 0:2 * D]).then_inc(g.d_gru, 16)
    for j in range(4):
        rows = a["L3_cond_W_hh"][64 * j:64 * j + 64, :].rearrange("(c f) n -> f c n", f=32)
        sp.dma_start(g.w_h[32 * j:32 * j + 32, :, :, :].rearrange("p c g n -> p c (g n)"), rows).then_inc(g.d_gru, 16)
    sp.wait_ge(g.zeroed3, 2)
    row = lambda v: v.rearrange("(o g n) -> o g n", o=1, n=D)
    sp.dma_start(g.bias3[0:1, 0:1, :], row(a["L3_cond_b_ih"])[:, 2:3, :]).then_inc(g.d_gru, 16)
    sp.dma_start(g.bias3[0:1, 1:3, :], row(a["L3_cond_b_ih"])[:, 0:2, :]).then_inc(g.d_gru, 16)
    sp.dma_start(g.bias3[1:2, 1:4, :], row(a["L3_cond_b_hh"])).then_inc(g.d_gru, 16)
    for j in range(4):
        sp.dma_start(g.h[0][32 * j:32 * j + B, :], a["cond_2048"][:, 64 * j:64 * j + 64]).then_inc(g.d_gru, 16)


class Shared:
    pass


def layers(nc, a, out):
    g = Shared()
    with ExitStack() as whole:
        def sb(ctx, name, shape, dt=F32):
            return ctx.enter_context(nc.sbuf_tensor(name, shape, dt))

        sem = lambda name: whole.enter_context(nc.semaphore(name))
        g.bank = [whole.enter_context(nc.psum_tensor(f"bank{i}", [P, 512], F32)) for i in range(8)]
        g.ident = sb(whole, "ident", [P, P])
        g.mean_w = sb(whole, "mean_w", [P, P])
        g.block_w = sb(whole, "block_w", [P, P])
        g.eps6 = sb(whole, "eps6", [P, 1])
        g.condT = sb(whole, "condT", [P, C, B])
        g.vec = sb(whole, "vec", [P, V_ROWS])
        g.coup_scale = sb(whole, "coup_scale", [P, 4])
        g.coup_hi = sb(whole, "coup_hi", [P, C * D], F16)
        g.coup_lo = sb(whole, "coup_lo", [P, C * D], F16)
        g.gain0 = sb(whole, "gain0", [P, C, B])
        g.shift0 = sb(whole, "shift0", [P, C, B])
        g.ada = sb(whole, "ada", [P, 6 * C, B])
        g.drive_b = sb(whole, "drive_b", [P, C])
        g.x2_flat = sb(whole, "x2", [P, C * TOK + T])
        g.x2 = g.x2_flat[:, 0:C * TOK].rearrange("p (c b t) -> p c b t", c=C, b=B)
        g.d_w0, g.d_ada = sem("d_w0"), sem("d_ada")
        g.d_w2, g.d_ow, g.d_ff = sem("d_w2"), sem("d_ow"), sem("d_ff")
        g.d_x3 = [sem(f"d_x3tok{i}") for i in range(2)]
        g.d_gru, g.zeroed3 = sem("d_gru"), sem("zeroed3")
        g.d_keep = sem("d_keep")
        g.d_vb = [sem(f"d_vb{i}") for i in range(4)]
        x3_dram = nc.dram_tensor("x3_tokens", [B, T, D], F32, kind="Internal").ap()
        x2_dram = nc.dram_tensor("x2_in", [P, C, B, T], F32, kind="Internal").ap()
        with ExitStack() as scan:
            g.x1 = sb(scan, "x1", [P, T, C, B])
            g.drive = sb(scan, "drive", [P, T + 1, C, B])
            with ExitStack() as layer0:
                g.w_out0 = sb(layer0, "w_out0", [P, C, D])
                g.w_qkv0 = sb(layer0, "w_qkv0", [P, C, 3 * D])
                g.ada_w = sb(layer0, "ada_w", [P, C, 6 * D])
                g.xT = sb(layer0, "xT", [P, C, B, T])
                g.xm = sb(layer0, "xm", [P, C, B, T])
                with ExitStack() as ctx:
                    prepare(nc, ctx, a, g)
                g.q0 = sb(layer0, "q0", [P, C, TOK])
                g.k0 = [sb(layer0, f"k0_{i}", [P, C, TOK]) for i in range(2)]
                g.v0 = sb(layer0, "v0", [P, 2, B, D])
                with ExitStack() as ctx:
                    project0(nc, ctx, a, g)
                with ExitStack() as ctx:
                    attend0(nc, ctx, a, g)
            g.trace = sb(scan, "trace", [P, T + 1, C, B])
            with ExitStack() as ctx:
                scan1(nc, ctx, a, g)
        with ExitStack() as layer2:
            xh = sb(layer2, "x_hi", [P, C, TOK], F32R)
            xl = sb(layer2, "x_lo", [P, C, TOK], F32R)
            with ExitStack() as heads:
                g.w_stage = sb(heads, "w2_stage", [P, 3, C, 512])
                g.ow_stage = sb(heads, "ow_stage", [P, 4, D])
                g.v_bias = sb(heads, "v_bias", [P, 2, 512])

                def loads(sp):
                    load_w2(sp, a, g, 0)
                    load_ow(sp, a, g, 0)
                    load_vb(sp, a, g, 0)
                    sp.dma_start(x2_dram, g.x2[:, :, :, :]).then_inc(g.d_keep, 16)
                    sp.wait_ge(g.d_keep, 16)

                with ExitStack() as ctx:
                    norm_split(nc, ctx, a, g, "_a", 1, 0, xh, xl, loads)
                with ExitStack() as ctx:
                    attend2(nc, ctx, a, g, xh, xl)
        with ExitStack() as last:
            gru_buffers(lambda name, shape: sb(last, name, shape), g)
            with ExitStack() as layer2:
                xh = sb(layer2, "x_hi_b", [P, C, TOK], F32R)
                xl = sb(layer2, "x_lo_b", [P, C, TOK], F32R)
                g.w1_stage = sb(layer2, "w1_stage", [P, C, FF])
                g.x2_in = sb(layer2, "x2_in_sb", [P, C, B, T])
                g.ffw2_stage = sb(layer2, "ffw2_stage", [P, FF // P, D])

                def loads(sp):
                    sp.dma_start(g.w1_stage[:, :, :],
                                 a["L2_cond_ffn_w1"].rearrange("(c p) n -> p c n", p=P)).then_inc(g.d_ff, 16)
                    sp.dma_start(g.ffw2_stage[:, :, :],
                                 a["L2_cond_ffn_w2"].rearrange("(k p) n -> p k n", p=P)).then_inc(g.d_ff, 16)
                    sp.dma_start(g.x2_in[:, :, :, :], x2_dram).then_inc(g.d_keep, 16)

                with ExitStack() as ctx:
                    norm_split(nc, ctx, a, g, "_b", 4, 3, xh, xl, loads)
                with ExitStack() as ctx:
                    feed_forward(nc, ctx, a, g, xh, xl, x3_dram)
            with ExitStack() as ctx:
                gru(nc, ctx, a, g, out, x3_dram)


_INS = ["x", "cond_2048", "L0_cond_W_emb", "L0_cond_b_emb", "L0_cond_g_norm", "L0_cond_W_qkv", "L0_cond_g_q",
        "L0_cond_g_k", "L0_cond_W_out", "L1_cond_coupling", "L1_cond_bias", "L2_cond_ada_w", "L2_cond_ada_b",
        "L2_cond_qkv_w", "L2_cond_qkv_b", "L2_cond_out_w", "L2_cond_out_b", "L2_cond_ffn_w1", "L2_cond_ffn_b1",
        "L2_cond_ffn_w2", "L2_cond_ffn_b2", "L3_cond_W_ih", "L3_cond_W_hh", "L3_cond_b_ih", "L3_cond_b_hh"]


def kernel(**inputs):
    import numpy as _np
    import concourse.bacc as _bacc
    from concourse import mybir as _mybir
    from concourse.bass_utils import run_bass_kernel_spmd as _run

    nc = _bacc.Bacc("TRN2", target_bir_lowering=False, num_devices=1)
    arrays, aps = {}, {}
    for name in _INS:
        a = _np.ascontiguousarray(inputs[name])
        arrays[f"in_{name}_dram"] = a
        aps[name] = nc.dram_tensor(f"in_{name}_dram", a.shape, _mybir.dt.from_np(a.dtype), kind="ExternalInput").ap()
    out = nc.dram_tensor("out_0_dram", (B, T, D), F32, kind="ExternalOutput").ap()
    layers(nc, aps, out)
    r = _run(nc, [arrays], core_ids=[0])
    return r.results[0]["out_0_dram"]
```
